# Optimizing a Trainium2 kernel written in Bass

```python
import numpy as np
import jax
import jax.numpy as jnp

def _softmax(x, axis=-1):
    return jax.nn.softmax(x, axis=axis)

def _gelu(x):
    return jax.nn.gelu(x, approximate=True)

def _silu(x):
    return jax.nn.silu(x)

def _sigmoid(x):
    return jax.nn.sigmoid(x)

def _layernorm(x, axis=-1, eps=1e-05):
    m = jnp.mean(x, axis=axis, keepdims=True)
    v = jnp.var(x, axis=axis, keepdims=True)
    return (x - m) / jnp.sqrt(v + eps)

def _scatter_add(tgt, idx, src, axis=0):
    return tgt.at[idx].add(src)

def _segment_sum(src, seg, n):
    return jax.ops.segment_sum(src, seg, n)
kernel_name = 'mk_gnn_preln_d2_gnn_r8_5885ff'

def setup_inputs(seed: int=0):
    np.random.seed(seed)
    _w = jnp.asarray

    def _rec_inputs():
        import jax
        import jax.numpy as jnp
        _gk = jax.random.key(seed)
        x = -7.329e-05 + 0.9999 * jax.random.normal(jax.random.fold_in(_gk, 1), (6250, 512), jnp.float32)
        _s = jax.random.randint(jax.random.fold_in(_gk, 2), (50000,), 0, 6250, jnp.int32)
        _d = jax.random.randint(jax.random.fold_in(_gk, 3), (50000,), 0, 6250, jnp.int32)
        _loop = jnp.arange(6250, dtype=jnp.int32)
        src = jnp.concatenate([_s, _d, _loop])
        dst = jnp.concatenate([_d, _s, _loop])
        _o = jnp.argsort(dst, stable=True)
        src = src[_o]
        dst = dst[_o]
        edge_weight = jax.random.uniform(jax.random.fold_in(_gk, 12), (106250,), jnp.float32, 0.0, 0.999998)
        return (x, src, dst, edge_weight)
    x, src, dst, edge_weight = _rec_inputs()

    def _L0_gnn_setup():
        import jax, jax.numpy as jnp
        import numpy as np
        N = 12500
        E = 100000
        IN_FEATS = 512
        N_HIDDEN = 128
        key = jax.random.key(seed)
        k1, k2, k3, k4, k5, k6 = jax.random.split(key, 6)
        inputs = jax.random.normal(k1, (N, IN_FEATS), dtype=jnp.float32)
        edge_index = jax.random.randint(k2, (2, E), 0, N, dtype=jnp.int64)
        edge_attr = jax.random.uniform(k3, (E,), dtype=jnp.float32)
        s_gcn = jnp.sqrt(6.0 / (IN_FEATS + N_HIDDEN)).astype(jnp.float32)
        W_gcn = jax.random.uniform(k4, (IN_FEATS, N_HIDDEN), dtype=jnp.float32, minval=-s_gcn, maxval=s_gcn)
        b_gcn = jnp.zeros((N_HIDDEN,), dtype=jnp.float32)
        s_fc = jnp.sqrt(6.0 / (N_HIDDEN + IN_FEATS)).astype(jnp.float32)
        W_fc = jax.random.uniform(k5, (IN_FEATS, N_HIDDEN), dtype=jnp.float32, minval=-s_fc, maxval=s_fc)
        b_fc = jax.random.uniform(k6, (IN_FEATS,), dtype=jnp.float32, minval=-1.0 / np.sqrt(N_HIDDEN), maxval=1.0 / np.sqrt(N_HIDDEN))
        return {'inputs': inputs, 'edge_index': edge_index, 'edge_attr': edge_attr, 'W_gcn': W_gcn, 'b_gcn': b_gcn, 'W_fc': W_fc, 'b_fc': b_fc}
    _L0_gnn_all = _L0_gnn_setup()
    _L0_gnn_in = {k: v for k, v in _L0_gnn_all.items() if k in ('W_gcn', 'b_gcn', 'W_fc', 'b_fc')}
    del _L0_gnn_all

    def _L1_gnn_setup():
        import jax, jax.numpy as jnp
        import numpy as np
        N_NODES = 5000
        N_EDGES = 80000
        DIM_H = 512
        N_HEADS = 8
        D_HEAD = DIM_H // N_HEADS

        def _exphormer_attn(x, edge_index, Wq, Wk, Wv):
            N, D = x.shape
            H, d = (N_HEADS, D_HEAD)
            Q = (x @ Wq).reshape(N, H, d)
            K = (x @ Wk).reshape(N, H, d)
            V = (x @ Wv).reshape(N, H, d)
            src, dst = (edge_index[0], edge_index[1])
            scale = np.float32(1.0 / np.sqrt(d))
            score = jnp.einsum('ehd,ehd->eh', K[src], Q[dst]) * scale
            score = jnp.exp(jnp.clip(score, -5.0, 5.0))[..., None]
            msg = V[src] * score
            wV = jax.ops.segment_sum(msg, dst, num_segments=N)
            Z = jax.ops.segment_sum(score, dst, num_segments=N)
            return (wV / (Z + 1e-06)).reshape(N, D)
        key = jax.random.key(seed)
        ks = jax.random.split(key, 8)
        x = jax.random.normal(ks[0], (N_NODES, DIM_H), dtype=jnp.float32)
        edge_index = jax.random.randint(ks[1], (2, N_EDGES), 0, N_NODES, dtype=jnp.int32)
        virt_h = jax.random.normal(ks[2], (1, DIM_H), dtype=jnp.float32)
        virt_edge_index = jnp.zeros((2, 1), dtype=jnp.int32)
        s = 1.0 / np.sqrt(DIM_H)
        Wq = jax.random.normal(ks[3], (DIM_H, DIM_H), dtype=jnp.float32) * s
        Wk = jax.random.normal(ks[4], (DIM_H, DIM_H), dtype=jnp.float32) * s
        Wv = jax.random.normal(ks[5], (DIM_H, DIM_H), dtype=jnp.float32) * s
        bn_gamma = jnp.ones((DIM_H,), dtype=jnp.float32)
        bn_beta = jnp.zeros((DIM_H,), dtype=jnp.float32)
        return {'x': x, 'edge_index': edge_index, 'virt_h': virt_h, 'virt_edge_index': virt_edge_index, 'Wq': Wq, 'Wk': Wk, 'Wv': Wv, 'bn_gamma': bn_gamma, 'bn_beta': bn_beta}
    _L1_gnn_all = _L1_gnn_setup()
    _L1_gnn_in = {k: v for k, v in _L1_gnn_all.items() if k in ('virt_h', 'virt_edge_index', 'Wq', 'Wk', 'Wv', 'bn_gamma', 'bn_beta')}
    del _L1_gnn_all
    return {'x': x, 'src': src, 'dst': dst, 'edge_weight': edge_weight, 'L0_gnn_W_gcn': _L0_gnn_in['W_gcn'], 'L0_gnn_b_gcn': _L0_gnn_in['b_gcn'], 'L0_gnn_W_fc': _L0_gnn_in['W_fc'], 'L0_gnn_b_fc': _L0_gnn_in['b_fc'], 'L1_gnn_virt_h': _L1_gnn_in['virt_h'], 'L1_gnn_virt_edge_index': _L1_gnn_in['virt_edge_index'], 'L1_gnn_Wq': _L1_gnn_in['Wq'], 'L1_gnn_Wk': _L1_gnn_in['Wk'], 'L1_gnn_Wv': _L1_gnn_in['Wv'], 'L1_gnn_bn_gamma': _L1_gnn_in['bn_gamma'], 'L1_gnn_bn_beta': _L1_gnn_in['bn_beta']}

def reference(x, src, dst, edge_weight, L0_gnn_W_gcn, L0_gnn_b_gcn, L0_gnn_W_fc, L0_gnn_b_fc, L1_gnn_virt_h, L1_gnn_virt_edge_index, L1_gnn_Wq, L1_gnn_Wk, L1_gnn_Wv, L1_gnn_bn_gamma, L1_gnn_bn_beta):
    import jax
    import jax.numpy as jnp

    def _L0_gnn_ref(inputs, edge_index, edge_attr, W_gcn, b_gcn, W_fc, b_fc):
        import jax, jax.numpy as jnp
        import numpy as np
        N = 12500
        E = 100000
        IN_FEATS = 512
        N_HIDDEN = 128
        x = inputs @ W_gcn
        src, dst = (edge_index[0], edge_index[1])
        msg = x[src] * edge_attr[:, None]
        h = jax.ops.segment_sum(msg, dst, num_segments=inputs.shape[0]) + b_gcn
        return h @ W_fc.T + b_fc

    def _L1_gnn_ref(x, edge_index, virt_h, virt_edge_index, Wq, Wk, Wv, bn_gamma, bn_beta):
        import jax, jax.numpy as jnp
        import numpy as np
        N_NODES = 5000
        N_EDGES = 80000
        DIM_H = 512
        N_HEADS = 8
        D_HEAD = DIM_H // N_HEADS

        def _exphormer_attn(x, edge_index, Wq, Wk, Wv):
            N, D = x.shape
            H, d = (N_HEADS, D_HEAD)
            Q = (x @ Wq).reshape(N, H, d)
            K = (x @ Wk).reshape(N, H, d)
            V = (x @ Wv).reshape(N, H, d)
            src, dst = (edge_index[0], edge_index[1])
            scale = np.float32(1.0 / np.sqrt(d))
            score = jnp.einsum('ehd,ehd->eh', K[src], Q[dst]) * scale
            score = jnp.exp(jnp.clip(score, -5.0, 5.0))[..., None]
            msg = V[src] * score
            wV = jax.ops.segment_sum(msg, dst, num_segments=N)
            Z = jax.ops.segment_sum(score, dst, num_segments=N)
            return (wV / (Z + 1e-06)).reshape(N, D)
        h_attn = _exphormer_attn(x, edge_index, Wq, Wk, Wv)
        h = x + h_attn
        mean = jnp.mean(h, axis=0)
        var = jnp.mean(jnp.square(h - mean), axis=0)
        return (h - mean) * jax.lax.rsqrt(var + 1e-05) * bn_gamma + bn_beta
    edge_index = jnp.stack([src, dst])
    h = jnp.maximum(_layernorm(x, axis=-1), 0.0)
    x = x + _L0_gnn_ref(h, edge_index, edge_weight, L0_gnn_W_gcn, L0_gnn_b_gcn, L0_gnn_W_fc, L0_gnn_b_fc)
    h = jnp.maximum(_layernorm(x, axis=-1), 0.0)
    x = x + _L1_gnn_ref(h, edge_index, L1_gnn_virt_h, L1_gnn_virt_edge_index, L1_gnn_Wq, L1_gnn_Wk, L1_gnn_Wv, L1_gnn_bn_gamma, L1_gnn_bn_beta)
    return x

_drawn_inputs = setup_inputs


def setup_inputs(seed=0):
    import zlib

    import numpy as np

    out = dict(_drawn_inputs(seed))
    spreads = {'L0_gnn_b_gcn': (0.0, 0.388),
     'L1_gnn_bn_gamma': (1.0, 0.2),
     'L1_gnn_bn_beta': (0.0, 0.296)}
    factors = {'L0_gnn_b_fc': 3.73}
    for name, (base, spread) in spreads.items():
        noise = np.random.default_rng([zlib.crc32(name.encode()), seed]).standard_normal(out[name].shape)
        drawn = base * np.exp(spread * noise) if base else spread * noise
        out[name] = jnp.asarray(drawn.astype(out[name].dtype))
    for name, factor in factors.items():
        out[name] = (out[name] * factor).astype(out[name].dtype)
    return out
```

```python
import concourse.bass as bass
from concourse import mybir
from contextlib import ExitStack

P = 128
CHUNK = 2 * P
RING = 4
f32, i32 = mybir.dt.float32, mybir.dt.int32
ALU = mybir.AluOpType
ACT = mybir.ActivationFunctionType
AX = mybir.AxisListType
LN_EPS, BN_EPS, Z_EPS = 1e-5, 1e-5, 1e-6
CLIP = 5.0


def shifted(turn, place, by):
    return turn + (place + by) // RING, (place + by) % RING


def run_steps(engine, count, ahead, behind, step):
    first = -(-(behind + RING) // RING)
    last = max(first, (count - ahead) // RING)
    for s in range(-ahead, RING * first if last > first else count + behind):
        step(s // RING, s % RING)
    if last > first:
        with engine.Fori(first, last) as turn:
            for place in range(RING):
                step(turn, place)
        for s in range(RING * last, count + behind):
            step(s // RING, s % RING)


class Item:

    def __init__(self, turn, place, by, count):
        self.turn, self.r = shifted(turn, place, by)
        self.fixed = isinstance(self.turn, int)
        self.n = self.turn * RING + self.r
        self.exists = not self.fixed or 0 <= self.n < count

    def wait(self, engine, sem, back=0, per=1):
        if not self.fixed or self.n - back >= 0:
            engine.wait_ge(sem, (self.n + (1 - back)) * per)

    def wait_ring(self, engine, sems, per, back=0):
        if not self.fixed or self.turn - back >= 0:
            engine.wait_ge(sems[self.r], (self.turn + (1 - back)) * per)


def build_program(nc, x, src, dst, edge_weight, W_gcn, b_gcn, W_fc, b_fc, Wq, Wk, Wv, gamma, beta, out):
    N, D = x.shape
    E = src.shape[0]
    HID = W_gcn.shape[1]
    HEADS = 8
    DH = D // HEADS
    KT = D // P
    NB = -(-N // P)
    TAIL = N - (NB - 1) * P
    NC = -(-E // CHUNK)
    NG = -(-NC // P)
    NS = NC + NB - 1
    AW = D + HEADS
    NONE = NB * P
    assert HID == P and NS <= 512 and D == 512

    ctx = ExitStack()
    with ctx:
        def sb(name, shape, dt=f32):
            return ctx.enter_context(nc.sbuf_tensor(name, shape, dt))

        def sem(name):
            return ctx.enter_context(nc.semaphore(name))

        def dram(name, shape):
            return nc.dram_tensor(name, shape, f32, kind="Internal").ap()

        xg_dram = dram("xg_rows", (NB * P, HID))
        kv_dram = dram("kv_rows", (NB * P, 2 * D))
        x1_dram = dram("x1_rows", (NB * P, D))
        h1_dram = dram("h1_rows", (NB * P, D))

        att = sb("att", [P, (NB + 1) * AW])
        rows_of = sb("rows_of", [P, NS, 2], i32)
        dst_in_block = sb("dst_in_block", [P, NS, 2])
        weight_of = sb("weight_of", [P, NS, 2])
        same_block = sb("same_block", [P, NS])
        block_of = sb("block_of", [1, NS], i32)
        column = sb("column", [P, P])
        ident = sb("ident", [P, P])
        ones = sb("ones", [P, P])
        gather_rows = sb("gather_rows", [P, RING, 2], i32)
        mean_var = sb("mean_var", [P, RING, 2])
        stats = sb("stats", [P, RING, 6])
        spread = sb("spread", [P, RING])
        scale = sb("scale", [P, RING])
        shift = sb("shift", [P, RING])
        eps_col = sb("eps_col", [P, 1])

        AGG = NB * P
        ARENA = AGG + KT * 3 * D + 2 * D + 2 * RING * D + 2 * D + 2 * 2 * D + RING * P + D
        arena = sb("arena", [P, ARENA])

        class Carver:
            def __init__(self, at=0):
                self.at = at

            def take(self, *shape):
                n = 1
                for s in shape:
                    n *= s
                assert self.at + n <= ARENA, "arena"
                v = arena[:, self.at:self.at + n]
                self.at += n
                if len(shape) == 2:
                    v = v.rearrange("p (a b) -> p a b", a=shape[0])
                if len(shape) == 3:
                    v = v.rearrange("p (a b c) -> p a b c", a=shape[0], b=shape[1])
                return v

        c = Carver()
        aggT = c.take(AGG)
        w_qkv = c.take(KT, 3 * D)
        w_fcT = c.take(D)
        bias_fc = c.take(D)
        xt = c.take(RING, D)
        ht = c.take(RING, D)
        hT = c.take(2, D)
        shared_at = c.at
        kv_out = c.take(2, 2 * D)
        hidden = c.take(RING, P)
        c = Carver(shared_at)
        xg_out = c.take(RING, HID)
        xg_in = c.take(RING, 2, HID)
        onehot_w = c.take(RING, 2, P)
        c = Carver(AGG)
        w_gcn = sb("w_gcn", [P, KT, HID])
        b_gcn_col = sb("b_gcn_col", [P, 1])
        w_fc_rows = c.take(KT, HID)

        c = Carver()
        kv_in = c.take(RING, 2, 2 * D)
        onehot = c.take(RING, 2, P)
        onehotT = c.take(2, 2, P)
        message = c.take(2, 2, D)
        product = c.take(2, D)
        score = c.take(2, 2, HEADS)
        weight = c.take(2, 2, HEADS)

        c = Carver()
        x1_in = c.take(RING, D)
        h1_in = c.take(RING, D)
        square = c.take(RING, D)
        recip_z = c.take(NB, HEADS)
        mean_b = c.take(D)
        scale_b = c.take(D)
        gamma_b = c.take(D)
        beta_b = c.take(D)

        class TableCarver(Carver):
            def take(self, *shape, dt=f32):
                n = 1
                for s in shape:
                    n *= s
                v = att[:, self.at:self.at + n]
                self.at += n
                if dt != f32:
                    v = v.bitcast(dt)
                if len(shape) == 2:
                    v = v.rearrange("p (a b) -> p a b", a=shape[0])
                return v

        c = TableCarver()
        dst_raw = c.take(NG, CHUNK, dt=i32)
        src_raw = c.take(NG, CHUNK, dt=i32)
        dst_rows = c.take(NG, CHUNK)
        src_rows = c.take(NG, CHUNK)
        w_rows = c.take(NG, CHUNK)
        slot_no = c.take(NS)
        chunk_of = c.take(NS)
        block_f = c.take(NS)
        block_base = c.take(NS)
        chunk_no = c.take(NG)
        chunk_end = c.take(NG)
        block_start = c.take(NB - 1)
        passed = c.take(NG, NB - 1)
        blocks_passed = c.take(NG)
        later = c.take(NG, NS)
        selects = c.take(NG, NS)
        partition_no = c.take(1)
        assert c.at <= (NB + 1) * AW

        bank = ctx.enter_context(nc.psum_tensor("bank", [P, 8, 512], f32))
        wide = bank[:, :, :].rearrange("p a b -> p (a b)")

        edges_in = sem("edges_in")
        weights_in = sem("weights_in")
        padded = sem("padded")
        iotas = sem("iotas")
        vec = sem("vec")
        consts_ready = sem("consts_ready")
        later_ready = sem("later_ready")
        chunk_counted = sem("chunk_counted")
        selects_ready = sem("selects_ready")
        tables_in_psum = sem("tables_in_psum")
        tables_ready = sem("tables_ready")
        fcT_in_psum = sem("fcT_in_psum")
        fcT_ready = sem("fcT_ready")
        w_qkv_in = sem("w_qkv_in")
        act_go = sem("act_go")
        pool_go = sem("pool_go")
        sp_go = sem("sp_go")
        vec_go = sem("vec_go")

        class NodeSems:
            def __init__(self, tag):
                self.x_in = [sem(f"{tag}_x_in{r}") for r in range(RING)]
                self.stats_done = sem(f"{tag}_stats_done")
                self.aggr_done = sem(f"{tag}_aggr_done")
                self.var_ready = sem(f"{tag}_var_ready")
                self.std_ready = sem(f"{tag}_std_ready")
                self.scale_ready = sem(f"{tag}_scale_ready")
                self.norm_ready = sem(f"{tag}_norm_ready")
                self.h_ready = sem(f"{tag}_h_ready")
                self.turned = sem(f"{tag}_turned")
                self.hT_ready = sem(f"{tag}_hT_ready")
                self.projected = sem(f"{tag}_projected")
                self.evacuated = sem(f"{tag}_evacuated")
                self.stored = [sem(f"{tag}_stored{r}") for r in range(RING)]

        n0, n1 = NodeSems("n0"), NodeSems("n1")
        hidden_ready = sem("hidden_ready")
        fc_done = sem("fc_done")
        x_biased = sem("x_biased")
        x1_ready = sem("x1_ready")
        q_evacuated = sem("q_evacuated")
        k_evacuated = sem("k_evacuated")
        rows_stored = [sem(f"rows_stored{r}") for r in range(RING)]
        att_cleared = sem("att_cleared")

        index_ready = sem("index_ready")
        xg_gathered = [sem(f"xg_gathered{r}") for r in range(RING)]
        onehot_w_ready = sem("onehot_w_ready")
        summed = sem("summed")
        added = sem("added")

        index2_ready = sem("index2_ready")
        kv_gathered = [sem(f"kv_gathered{r}") for r in range(RING)]
        onehot_ready = sem("onehot_ready")
        onehot_turned = sem("onehot_turned")
        onehotT_ready = sem("onehotT_ready")
        queries_ready = sem("queries_ready")
        product_ready = sem("product_ready")
        score_ready = sem("score_ready")
        clipped = sem("clipped")
        weight_ready = sem("weight_ready")
        message0_ready = sem("message0_ready")
        message1_ready = sem("message1_ready")
        att_summed = sem("att_summed")
        att_added = sem("att_added")

        norm_in = sem("norm_in")
        z_ready = sem("z_ready")
        h1_back = [sem(f"h1_back{r}") for r in range(RING)]
        x1_back = [sem(f"x1_back{r}") for r in range(RING)]
        attended = sem("attended")
        with_h = sem("with_h")
        mean_summed = sem("mean_summed")
        mean_ready = sem("mean_ready")
        centered = sem("centered")
        squared = sem("squared")
        square_read = sem("square_read")
        var_summed = sem("var_summed")
        bn_var_ready = sem("bn_var_ready")
        bn_std_ready = sem("bn_std_ready")
        x1_biased = sem("x1_biased")
        scaled = sem("scaled")
        y_ready = sem("y_ready")
        y_stored = [sem(f"y_stored{r}") for r in range(RING)]

        block = ctx.enter_context(nc.Block())

        FULL = E // CHUNK
        G_FULL = FULL // P
        REST = FULL - G_FULL * P
        ODD = E - FULL * CHUNK

        def load_chunks(engine, to, frm):
            n = 0
            if G_FULL:
                engine.dma_start(to[:, 0:G_FULL, :], frm[0:G_FULL * P * CHUNK].rearrange(
                    "(g p k) -> p g k", g=G_FULL, p=P)).then_inc(edges_in, 16)
                n += 1
            if REST:
                engine.dma_start(to[0:REST, G_FULL, :], frm[G_FULL * P * CHUNK:FULL * CHUNK].rearrange(
                    "(p k) -> p k", k=CHUNK)).then_inc(edges_in, 16)
                n += 1
            if ODD:
                engine.dma_start(to[REST:REST + 1, G_FULL, 0:ODD],
                                 frm[FULL * CHUNK:E].rearrange("(p k) -> p k", p=1)).then_inc(edges_in, 16)
                n += 1
            return n

        LOADS = 3 * ((G_FULL > 0) + (REST > 0) + (ODD > 0))

        def node_rows(t, n):
            if isinstance(n, int):
                return t[n * P:min(N, (n + 1) * P), :] if t is x or t is out else t[n * P:(n + 1) * P, :]
            return t[bass.ds(n * P, P), :]

        def used(t, n, tile):
            if isinstance(n, int) and (t is x or t is out):
                return tile[0:min(P, N - n * P)]
            return tile

        def message_of(it, t):
            heads = lambda v: v.rearrange("p (h d) -> p h d", h=HEADS)
            return (heads(message[:, it.r % 2, t, :]), heads(kv_in[:, it.r, t, D:2 * D]),
                    weight[:, it.r % 2, t, :].unsqueeze(2).broadcast_to([P, HEADS, DH]))

        def slot_column(table, it, t=None):
            flat = table[:, :, :].rearrange("p j t -> p (j t)")
            at, n = (it.n * 2, 2) if t is None else (it.n * 2 + t, 1)
            return flat[:, at:at + n] if it.fixed else flat[:, bass.ds(at, n)]

        def slot_scalar(table, it):
            return table[:, it.n:it.n + 1] if it.fixed else table[:, bass.ds(it.n, 1)]

        def slot_block(engine, it):
            at = block_of[0:1, it.n:it.n + 1] if it.fixed else block_of[0:1, bass.ds(it.n, 1)]
            return engine.value_load(at, min_val=0, max_val=NB - 1)

        @block.sync
        def _(sp):
            sp.wait_ge(padded, 3)
            load_chunks(sp, dst_raw, dst)
            load_chunks(sp, src_raw, src)
            load_chunks(sp, w_rows, edge_weight)
            sp.dma_start(w_gcn[:, :, :], W_gcn.rearrange("(k p) n -> p k n", p=P)).then_inc(weights_in, 16)
            sp.dma_start(w_fc_rows, W_fc.rearrange("(k p) n -> p k n", p=P)).then_inc(weights_in, 16)
            sp.dma_start(b_gcn_col[:, :], b_gcn.rearrange("(p a) -> p a", a=1)).then_inc(weights_in, 16)
            sp.dma_start(bias_fc, b_fc.rearrange("(a n) -> a n", a=1).broadcast_to([P, D])).then_inc(weights_in, 16)

            def step0(turn, place):
                it = Item(turn, place, 2, NB)
                if it.exists:
                    it.wait(sp, n0.h_ready, back=RING)
                    sp.sem_inc(sp_go, 1)
                    sp.dma_start(used(x, it.n, xt[:, it.r, :]), node_rows(x, it.n)).then_inc(n0.x_in[it.r], 16)
                it = Item(turn, place, -4, NB)
                if it.exists:
                    it.wait(sp, n0.evacuated)
                    sp.sem_inc(sp_go, 1)
                    sp.dma_start(node_rows(xg_dram, it.n), xg_out[:, it.r, :]).then_inc(n0.stored[it.r], 16)

            run_steps(sp, NB, 2, 4, step0)

            sp.wait_ge(fcT_in_psum, 1)
            for i, w in enumerate((Wq, Wk, Wv)):
                sp.dma_start(w_qkv[:, :, i * D:(i + 1) * D],
                             w.rearrange("(k p) n -> p k n", p=P)).then_inc(w_qkv_in, 16)

            def step1(turn, place):
                it = Item(turn, place, 2, NB)
                if it.exists:
                    it.wait_ring(sp, rows_stored, 32, back=1)
                    sp.sem_inc(sp_go, 1)
                    it.wait(sp, n1.h_ready, back=RING)
                    sp.sem_inc(sp_go, 1)
                    sp.dma_start(used(x, it.n, xt[:, it.r, :]), node_rows(x, it.n)).then_inc(n1.x_in[it.r], 16)
                it = Item(turn, place, -1, NB)
                if it.exists:
                    it.wait(sp, n1.h_ready)
                    sp.sem_inc(sp_go, 1)
                    sp.dma_start(node_rows(x1_dram, it.n), xt[:, it.r, :]).then_inc(rows_stored[it.r], 16)
                    sp.dma_start(node_rows(h1_dram, it.n), ht[:, it.r, :]).then_inc(rows_stored[it.r], 16)
                it = Item(turn, place, -4, NB)
                if it.exists:
                    it.wait(sp, n1.evacuated)
                    sp.sem_inc(sp_go, 1)
                    it.wait(sp, k_evacuated)
                    sp.sem_inc(sp_go, 1)
                    sp.dma_start(node_rows(kv_dram, it.n), kv_out[:, it.r % 2, :]).then_inc(n1.stored[it.r], 16)

            sp.wait_ge(n0.h_ready, NB)
            run_steps(sp, NB, 2, 4, step1)

            sp.wait_ge(att_added, NS)
            for r in range(RING):
                sp.wait_ge(rows_stored[r], 32 * len(range(r, NB, RING)))
            sp.dma_start(gamma_b, gamma.rearrange("(a n) -> a n", a=1).broadcast_to([P, D])).then_inc(norm_in, 16)
            sp.dma_start(beta_b, beta.rearrange("(a n) -> a n", a=1).broadcast_to([P, D])).then_inc(norm_in, 16)

            def step_h(turn, place):
                it = Item(turn, place, 2, NB)
                if it.exists:
                    it.wait(sp, with_h, back=RING)
                    sp.sem_inc(sp_go, 1)
                    sp.dma_start(h1_in[:, it.r, :], node_rows(h1_dram, it.n)).then_inc(h1_back[it.r], 16)

            run_steps(sp, NB, 2, 0, step_h)

            def step_y(turn, place):
                it = Item(turn, place, 2, NB)
                if it.exists:
                    it.wait_ring(sp, y_stored, 16, back=1)
                    sp.sem_inc(sp_go, 1)
                    sp.dma_start(x1_in[:, it.r, :], node_rows(x1_dram, it.n)).then_inc(x1_back[it.r], 16)
                it = Item(turn, place, -1, NB)
                if it.exists:
                    it.wait(sp, y_ready)
                    sp.sem_inc(sp_go, 1)
                    sp.dma_start(node_rows(out, it.n), used(out, it.n, x1_in[:, it.r, :])).then_inc(y_stored[it.r], 16)

            run_steps(sp, NB, 2, 1, step_y)
            for r in range(RING):
                sp.wait_ge(y_stored[r], 16 * len(range(r, NB, RING)))

        @block.gpsimd
        def _(pool):
            nc.gpsimd.memset(dst_raw, NONE).then_inc(padded, 1)
            nc.gpsimd.memset(src_raw, 0).then_inc(padded, 1)
            nc.gpsimd.memset(w_rows, 0.0).then_inc(padded, 1)
            free = dict(allow_small_or_imprecise_dtypes=True)
            nc.gpsimd.iota(column[:, :], pattern=[[1, P]], base=0, channel_multiplier=0, **free).then_inc(iotas, 1)
            nc.gpsimd.iota(partition_no, pattern=[[0, 1]], base=0, channel_multiplier=1, **free).then_inc(iotas, 1)
            nc.gpsimd.iota(slot_no, pattern=[[1, NS]], base=0, channel_multiplier=0, **free).then_inc(iotas, 1)
            nc.gpsimd.iota(chunk_no, pattern=[[P, NG]], base=0, channel_multiplier=1, **free).then_inc(iotas, 1)
            nc.gpsimd.iota(block_start, pattern=[[P, NB - 1]], base=P, channel_multiplier=0, **free).then_inc(iotas, 1)

            for r in range(RING):
                pool.wait_ge(n0.stored[r], 16 * len(range(r, NB, RING)))

            def gather0(turn, place):
                it = Item(turn, place, 0, NS)
                it.wait(pool, index_ready)
                it.wait(pool, summed, back=RING)
                pool.sem_inc(pool_go, 1)
                for t in range(2):
                    pool.indirect_dma_start(
                        out=xg_in[:, it.r, t, :], out_offset=None, in_=xg_dram,
                        in_offset=bass.IndirectOffsetOnAxis(ap=gather_rows[:, it.r, t:t + 1], axis=0),
                    ).then_inc(xg_gathered[it.r], 16)

            run_steps(pool, NS, 0, 0, gather0)

            pool.wait_ge(weights_in, 64)

            def bias(turn, place):
                it = Item(turn, place, 1, NB)
                if it.exists:
                    it.wait_ring(pool, n1.x_in, 16)
                    nc.gpsimd.tensor_tensor(xt[:, it.r, :], xt[:, it.r, :], bias_fc, ALU.add).then_inc(x_biased, 1)

            run_steps(pool, NB, 1, 0, bias)

            for r in range(RING):
                pool.wait_ge(n1.stored[r], 16 * len(range(r, NB, RING)))
                pool.wait_ge(rows_stored[r], 32 * len(range(r, NB, RING)))

            def step2(turn, place):
                it = Item(turn, place, 2, NS)
                if it.exists:
                    it.wait(pool, index2_ready)
                    it.wait(pool, message1_ready, back=RING)
                    it.wait(pool, message0_ready, back=RING)
                    pool.sem_inc(pool_go, 1)
                    for t in range(2):
                        pool.indirect_dma_start(
                            out=kv_in[:, it.r, t, :], out_offset=None, in_=kv_dram,
                            in_offset=bass.IndirectOffsetOnAxis(ap=gather_rows[:, it.r, t:t + 1], axis=0),
                        ).then_inc(kv_gathered[it.r], 16)
                it = Item(turn, place, -1, NS)
                if it.exists:
                    it.wait(pool, weight_ready)
                    it.wait(pool, att_summed, back=2)
                    nc.gpsimd.tensor_tensor(*message_of(it, 0), ALU.mult).then_inc(message0_ready, 1)

            run_steps(pool, NS, 2, 1, step2)

            pool.wait_ge(norm_in, 32)

            def bias2(turn, place):
                it = Item(turn, place, 1, NB)
                if it.exists:
                    it.wait_ring(pool, x1_back, 16)
                    nc.gpsimd.tensor_tensor(x1_in[:, it.r, :], x1_in[:, it.r, :], beta_b, ALU.add).then_inc(x1_biased, 1)

            run_steps(pool, NB, 1, 0, bias2)

        def node_act(act, s, turn, place):
            it = Item(turn, place, 0, NB)
            if it.exists:
                it.wait(act, s.var_ready)
                nc.scalar.activation(scale[:, it.r:it.r + 1], spread[:, it.r:it.r + 1], ACT.Sqrt).then_inc(s.std_ready, 1)
            it = Item(turn, place, -1, NB)
            if it.exists:
                it.wait(act, s.norm_ready)
                it.wait(act, s.turned, back=RING)
                if s is n1:
                    it.wait_ring(act, rows_stored, 32, back=1)
                nc.scalar.activation(ht[:, it.r, :], xt[:, it.r, :], ACT.Relu, bias=shift[:, it.r:it.r + 1],
                                     scale=scale[:, it.r:it.r + 1]).then_inc(s.h_ready, 1)
            it = Item(turn, place, -2, NB)
            if it.exists:
                it.wait(act, s.turned)
                it.wait(act, s.projected, back=2)
                nc.scalar.activation(hT[:, it.r % 2, :], bank[:, it.r % 2 if s is n0 else 1, :],
                                     ACT.Copy).then_inc(s.hT_ready, 1)

        @block.scalar
        def _(act):
            run_steps(act, NB, 0, 2, lambda turn, place: node_act(act, n0, turn, place))

            act.wait_ge(tables_ready, 1)

            def index0(turn, place):
                it = Item(turn, place, 0, NS)
                it.wait_ring(act, xg_gathered, 32, back=1)
                act.sem_inc(act_go, 1)
                nc.scalar.activation(gather_rows[:, it.r, :], slot_column(rows_of, it), ACT.Copy).then_inc(index_ready, 1)

            run_steps(act, NS, 0, 0, index0)

            act.wait_ge(added, NS)
            act.wait_ge(weights_in, 64)

            def step1(turn, place):
                it = Item(turn, place, 1, NB)
                if it.exists:
                    it.wait(act, fc_done, back=RING)
                    act.sem_inc(act_go, 1)
                    nc.scalar.activation(hidden[:, it.r, :], aggT[:, it.n * P:(it.n + 1) * P] if it.fixed
                                         else aggT[:, bass.ds(it.n * P, P)], ACT.Identity,
                                         bias=b_gcn_col[:, :]).then_inc(hidden_ready, 1)
                node_act(act, n1, turn, place)
                it = Item(turn, place, -4, NB)
                if it.exists:
                    it.wait(act, n1.projected)
                    act.sem_inc(act_go, 1)
                    at = (it.n + 1) * AW
                    nc.scalar.activation(att[:, at:at + D] if it.fixed else att[:, bass.ds(at, D)],
                                         bank[:, 2 + 3 * (it.r % 2), :], ACT.Copy).then_inc(q_evacuated, 1)
                    if not it.fixed or it.n >= 2:
                        two = Item(turn, place, -6, NB)
                        two.wait_ring(act, n1.stored, 16)
                    nc.scalar.activation(kv_out[:, it.r % 2, 0:D], bank[:, 3 + 3 * (it.r % 2), :],
                                         ACT.Copy).then_inc(k_evacuated, 1)

            run_steps(act, NB, 1, 4, step1)

            for r in range(RING):
                act.wait_ge(n1.stored[r], 16 * len(range(r, NB, RING)))
                act.wait_ge(rows_stored[r], 32 * len(range(r, NB, RING)))

            def step2(turn, place):
                it = Item(turn, place, 3, NS)
                if it.exists:
                    it.wait_ring(act, kv_gathered, 32, back=1)
                    act.sem_inc(act_go, 1)
                    nc.scalar.activation(gather_rows[:, it.r, :], slot_column(rows_of, it),
                                         ACT.Copy).then_inc(index2_ready, 1)
                it = Item(turn, place, 2, NS)
                if it.exists:
                    it.wait(act, onehot_turned)
                    it.wait(act, queries_ready, back=2)
                    nc.scalar.activation(onehotT[:, it.r % 2, :, :], bank[:, 6 + it.r % 2, 0:CHUNK].rearrange(
                        "p (t e) -> p t e", t=2), ACT.Copy).then_inc(onehotT_ready, 1)
                it = Item(turn, place, 0, NS)
                if it.exists:
                    it.wait(act, clipped)
                    it.wait(act, att_summed, back=2)
                    nc.scalar.activation(weight[:, it.r % 2, :, :], score[:, it.r % 2, :, :], ACT.Exp,
                                         scale=DH ** -0.5).then_inc(weight_ready, 1)

            run_steps(act, NS, 3, 0, step2)

            def squares(turn, place):
                it = Item(turn, place, 0, NB)
                it.wait(act, centered)
                it.wait(act, square_read, back=RING)
                act.sem_inc(act_go, 1)
                at = it.n * AW
                nc.scalar.activation(square[:, it.r, :], att[:, at:at + D] if it.fixed else att[:, bass.ds(at, D)],
                                     ACT.Square).then_inc(squared, 1)

            run_steps(act, NB, 0, 0, squares)
            act.wait_ge(bn_var_ready, 1)
            nc.scalar.activation(scale_b, scale_b, ACT.Sqrt).then_inc(bn_std_ready, 1)

        @block.vector
        def _(dve):
            steps = [0]

            def link(instruction):
                steps[0] += 1
                instruction.then_inc(vec, 1)
                dve.wait_ge(vec, steps[0])

            nc.vector.memset(ones[:, :], 1.0)
            link(nc.vector.memset(aggT, 0.0))
            dve.wait_ge(iotas, 5)
            nc.vector.tensor_scalar(ident[:, :], column[:, :], partition_no, None, ALU.is_equal).then_inc(consts_ready, 1)

            dve.wait_ge(edges_in, 16 * LOADS)
            nc.vector.tensor_copy(src_rows, src_raw)
            link(nc.vector.tensor_copy(dst_rows, dst_raw))
            last_dst = dst_rows[:, :, CHUNK - 1:CHUNK]
            link(nc.vector.tensor_tensor(passed, last_dst.broadcast_to([P, NG, NB - 1]),
                                         block_start.unsqueeze(1).broadcast_to([P, NG, NB - 1]), ALU.is_ge))
            link(nc.vector.tensor_reduce(blocks_passed, passed, AX.X, ALU.add))
            link(nc.vector.tensor_tensor(chunk_end, blocks_passed, chunk_no, ALU.add))
            for g in range(NG):
                last = nc.vector.tensor_scalar(later[:, g, :], slot_no, chunk_end[:, g:g + 1], None, ALU.is_gt)
            last.then_inc(later_ready, 1)
            dve.wait_ge(chunk_counted, 1)
            link(nc.vector.tensor_copy(chunk_of, bank[:, 0, 0:NS]))
            for g in range(NG):
                last = nc.vector.tensor_scalar(selects[:, g, :], chunk_of, chunk_no[:, g:g + 1], None, ALU.is_equal)
            last.then_inc(selects_ready, 1)
            link(nc.vector.tensor_tensor(block_f, slot_no, chunk_of, ALU.subtract))
            nc.vector.tensor_scalar(block_base, block_f, float(P), None, ALU.mult)
            nc.vector.tensor_copy(block_of[:, :], block_f[0:1, :])
            nc.vector.memset(same_block[:, 0:1], 0.0)
            link(nc.vector.tensor_tensor(same_block[:, 1:NS], block_f[:, 1:NS], block_f[:, 0:NS - 1], ALU.is_equal))
            dve.wait_ge(tables_in_psum, 1)
            for t in range(2):
                nc.vector.tensor_tensor(dst_in_block[:, :, t], bank[:, 1 + t, 0:NS], block_base, ALU.subtract)
                nc.vector.tensor_copy(rows_of[:, :, t], bank[:, 3 + t, 0:NS])
                last = nc.vector.tensor_copy(weight_of[:, :, t], bank[:, 5 + t, 0:NS])
            last.then_inc(tables_ready, 1)
            dve.wait_ge(tables_ready, 1)
            dve.wait_ge(fcT_in_psum, 1)
            nc.vector.tensor_copy(w_fcT, bank[:, 7, :]).then_inc(fcT_ready, 1)

            def node_stats(s, turn, place):
                it = Item(turn, place, 0, NB)
                if it.exists:
                    if s is n0:
                        it.wait_ring(dve, s.x_in, 16)
                    else:
                        it.wait(dve, x1_ready)
                    it.wait(dve, s.h_ready, back=RING)
                    nc.vector.bn_stats(stats[:, it.r, :], xt[:, it.r, :]).then_inc(s.stats_done, 1)
                    it.wait(dve, s.stats_done)
                    dve.sem_inc(vec_go, 1)
                    nc.vector.bn_aggr(mean_var[:, it.r, :], stats[:, it.r, :]).then_inc(s.aggr_done, 1)
                    it.wait(dve, s.aggr_done)
                    nc.vector.tensor_scalar(spread[:, it.r:it.r + 1], mean_var[:, it.r, 1:2], LN_EPS, None,
                                            ALU.add).then_inc(s.var_ready, 1)
                it = Item(turn, place, -1, NB)
                if it.exists:
                    it.wait(dve, s.std_ready)
                    nc.vector.reciprocal(scale[:, it.r:it.r + 1], scale[:, it.r:it.r + 1]).then_inc(s.scale_ready, 1)
                    it.wait(dve, s.scale_ready)
                    nc.vector.scalar_tensor_tensor(shift[:, it.r:it.r + 1], mean_var[:, it.r, 0:1], -1.0,
                                                   scale[:, it.r:it.r + 1], ALU.mult, ALU.mult).then_inc(s.norm_ready, 1)

            def step0(turn, place):
                node_stats(n0, turn, place)
                it = Item(turn, place, -3, NB)
                if it.exists:
                    it.wait(dve, n0.projected)
                    it.wait_ring(dve, n0.stored, 16, back=1)
                    nc.vector.tensor_copy(xg_out[:, it.r, :], bank[:, 2 + it.r % 2, 0:HID]).then_inc(n0.evacuated, 1)

            run_steps(dve, NB, 0, 3, step0)
            sums = att[:, :].rearrange("p (b w) -> p b w", w=AW)
            nc.vector.memset(sums[:, :, D:AW], 0.0)
            link(nc.vector.memset(sums[:, 0:1, 0:D], 0.0))

            for r in range(RING):
                dve.wait_ge(n0.stored[r], 16 * len(range(r, NB, RING)))

            def edges0(turn, place):
                it = Item(turn, place, 1, NS)
                if it.exists:
                    it.wait(dve, summed, back=RING)
                    for t in range(2):
                        last = nc.vector.tensor_scalar(onehot_w[:, it.r, t, :], column[:, :],
                                                       slot_column(dst_in_block, it, t), slot_column(weight_of, it, t),
                                                       ALU.is_equal, ALU.mult)
                    last.then_inc(onehot_w_ready, 1)
                it = Item(turn, place, -1, NS)
                if it.exists:
                    b = slot_block(dve, it)
                    it.wait(dve, summed)
                    it.wait(dve, added, back=1)
                    to = aggT[:, bass.ds(b * P, P)]
                    nc.vector.tensor_tensor(to, to, bank[:, it.r % 2, 0:P], ALU.add).then_inc(added, 1)

            run_steps(dve, NS, 1, 1, edges0)

            def step1(turn, place):
                it = Item(turn, place, 0, NB)
                if it.exists:
                    it.wait(dve, fc_done)
                    it.wait(dve, x_biased)
                    nc.vector.tensor_tensor(xt[:, it.r, :], xt[:, it.r, :], bank[:, 0, :], ALU.add).then_inc(x1_ready, 1)
                node_stats(n1, turn, place)
                it = Item(turn, place, -4, NB)
                if it.exists:
                    it.wait(dve, n1.projected)
                    if not it.fixed or it.n >= 2:
                        two = Item(turn, place, -6, NB)
                        two.wait_ring(dve, n1.stored, 16)
                    nc.vector.tensor_copy(kv_out[:, it.r % 2, D:2 * D],
                                          bank[:, 4 + 3 * (it.r % 2), :]).then_inc(n1.evacuated, 1)

            run_steps(dve, NB, 0, 4, step1)

            for r in range(RING):
                dve.wait_ge(n1.stored[r], 16 * len(range(r, NB, RING)))
                dve.wait_ge(rows_stored[r], 32 * len(range(r, NB, RING)))

            def step2(turn, place):
                it = Item(turn, place, -2, NS)
                if it.exists:
                    b = slot_block(dve, it)
                    it.wait(dve, att_summed)
                    it.wait(dve, att_added, back=1)
                    to = att[:, bass.ds(b * AW, AW)]
                    nc.vector.scalar_tensor_tensor(to, to, slot_scalar(same_block, it), wide[:, 4 * 512:4 * 512 + AW],
                                                   ALU.mult, ALU.add).then_inc(att_added, 1)
                it = Item(turn, place, 2, NS)
                if it.exists:
                    for t in range(2):
                        last = nc.vector.tensor_scalar(onehot[:, it.r, t, :], column[:, :],
                                                       slot_column(dst_in_block, it, t), None, ALU.is_equal)
                    last.then_inc(onehot_ready, 1)
                it = Item(turn, place, -1, NS)
                if it.exists:
                    it.wait(dve, weight_ready)
                    nc.vector.tensor_tensor(*message_of(it, 1), ALU.mult).then_inc(message1_ready, 1)
                it = Item(turn, place, 0, NS)
                if it.exists:
                    it.wait_ring(dve, kv_gathered, 32)
                    it.wait(dve, queries_ready)
                    nc.vector.tensor_tensor(product, kv_in[:, it.r, :, 0:D], bank[:, 2 * (it.r % 2):2 * (it.r % 2) + 2, :],
                                            ALU.mult).then_inc(product_ready, 1)
                    it.wait(dve, product_ready)
                    nc.vector.tensor_reduce(score[:, it.r % 2, :, :].rearrange("p t h -> p (t h)"),
                                            product.rearrange("p t (h d) -> p (t h) d", h=HEADS),
                                            AX.X, ALU.add).then_inc(score_ready, 1)
                    it.wait(dve, score_ready)
                    flat = score[:, it.r % 2, :, :]
                    limit = CLIP * DH ** 0.5
                    nc.vector.tensor_scalar(flat, flat, -limit, limit, ALU.max, ALU.min).then_inc(clipped, 1)

            run_steps(dve, NS, 2, 2, step2)

            dve.wait_ge(att_added, NS)
            z = sums[:, 0:NB, D:AW]
            link(nc.vector.tensor_scalar(recip_z, z, Z_EPS, None, ALU.add))
            link(nc.vector.reciprocal(recip_z, recip_z))
            flat_z = recip_z.rearrange("p b h -> p (b h)")

            def row(it):
                return att[:, it.n * AW:it.n * AW + D] if it.fixed else att[:, bass.ds(it.n * AW, D)]

            def attend(turn, place):
                it = Item(turn, place, 0, NB)
                v = row(it).rearrange("p (h d) -> p h d", h=HEADS)
                rz = flat_z[:, it.n * HEADS:(it.n + 1) * HEADS] if it.fixed else flat_z[:, bass.ds(it.n * HEADS, HEADS)]
                nc.vector.tensor_tensor(v, v, rz.unsqueeze(2).broadcast_to([P, HEADS, DH]), ALU.mult).then_inc(attended, 1)
                it.wait_ring(dve, h1_back, 16)
                it.wait(dve, attended)
                nc.vector.tensor_tensor(row(it), row(it), h1_in[:, it.r, :], ALU.add).then_inc(with_h, 1)

            run_steps(dve, NB, 0, 0, attend)
            dve.wait_ge(mean_summed, 1)
            link(nc.vector.tensor_scalar(mean_b, bank[:, 0, :], 1.0 / N, None, ALU.mult))

            def center(turn, place):
                it = Item(turn, place, 0, NB)
                nc.vector.tensor_tensor(row(it), row(it), mean_b, ALU.subtract).then_inc(centered, 1)

            run_steps(dve, NB, 0, 0, center)
            dve.wait_ge(var_summed, 1)
            nc.vector.tensor_scalar(scale_b, bank[:, 1, :], 1.0 / N, BN_EPS, ALU.mult, ALU.add).then_inc(bn_var_ready, 1)
            dve.wait_ge(bn_std_ready, 1)
            link(nc.vector.reciprocal(scale_b, scale_b))
            dve.wait_ge(norm_in, 32)
            link(nc.vector.tensor_tensor(scale_b, scale_b, gamma_b, ALU.mult))

            def finish(turn, place):
                it = Item(turn, place, 0, NB)
                nc.vector.tensor_tensor(row(it), row(it), scale_b, ALU.mult).then_inc(scaled, 1)
                it.wait(dve, scaled)
                it.wait(dve, x1_biased)
                nc.vector.tensor_tensor(x1_in[:, it.r, :], row(it), x1_in[:, it.r, :], ALU.add).then_inc(y_ready, 1)

            run_steps(dve, NB, 0, 0, finish)

        @block.tensor
        def _(pe):
            def turn_rows(s, it, to):
                for k in range(KT):
                    last = nc.tensor.transpose(to[:, k * P:(k + 1) * P], ht[:, it.r, k * P:(k + 1) * P], ident[:, :])
                last.then_inc(s.turned, 1)

            pe.wait_ge(later_ready, 1)
            for g in range(NG):
                last = nc.tensor.matmul(bank[:, 0, 0:NS], ones[:, :], later[:, g, :], start=(g == 0), stop=(g == NG - 1))
            last.then_inc(chunk_counted, 1)
            pe.wait_ge(selects_ready, 1)
            for a, rows in enumerate((dst_rows, src_rows, w_rows)):
                for t in range(2):
                    for g in range(NG):
                        last = nc.tensor.matmul(bank[:, 1 + 2 * a + t, 0:NS], rows[:, g, t * P:(t + 1) * P],
                                                selects[:, g, :], start=(g == 0), stop=(g == NG - 1))
            last.then_inc(tables_in_psum, 1)
            pe.wait_ge(weights_in, 64)
            for k in range(KT):
                last = nc.tensor.transpose(bank[:, 7, k * P:(k + 1) * P], w_fc_rows[:, k, :], ident[:, :])
            last.then_inc(fcT_in_psum, 1)
            pe.wait_ge(tables_ready, 1)

            def step0(turn, place):
                it = Item(turn, place, -1, NB)
                if it.exists:
                    it.wait(pe, n0.h_ready)
                    it.wait(pe, n0.hT_ready, back=2)
                    turn_rows(n0, it, bank[:, it.r % 2, :])
                it = Item(turn, place, -2, NB)
                if it.exists:
                    it.wait(pe, n0.hT_ready)
                    it.wait(pe, n0.evacuated, back=2)
                    for k in range(KT):
                        last = nc.tensor.matmul(bank[:, 2 + it.r % 2, 0:HID], hT[:, it.r % 2, k * P:(k + 1) * P],
                                                w_gcn[:, k, :], start=(k == 0), stop=(k == KT - 1))
                    last.then_inc(n0.projected, 1)

            run_steps(pe, NB, 0, 2, step0)

            def edges0(turn, place):
                it = Item(turn, place, 0, NS)
                it.wait_ring(pe, xg_gathered, 32)
                it.wait(pe, onehot_w_ready)
                it.wait(pe, added, back=2)
                for t in range(2):
                    last = nc.tensor.matmul(bank[:, it.r % 2, 0:P], xg_in[:, it.r, t, :], onehot_w[:, it.r, t, :],
                                            start=(t == 0), stop=(t == 1))
                last.then_inc(summed, 1)

            run_steps(pe, NS, 0, 0, edges0)
            pe.wait_ge(fcT_ready, 1)
            pe.wait_ge(w_qkv_in, 48)

            def step1(turn, place):
                it = Item(turn, place, 1, NB)
                if it.exists:
                    it.wait(pe, hidden_ready)
                    it.wait(pe, x1_ready, back=1)
                    nc.tensor.matmul(bank[:, 0, :], hidden[:, it.r, :], w_fcT, start=True, stop=True).then_inc(fc_done, 1)
                it = Item(turn, place, -2, NB)
                if it.exists:
                    it.wait(pe, n1.h_ready)
                    it.wait(pe, n1.hT_ready, back=1)
                    turn_rows(n1, it, bank[:, 1, :])
                it = Item(turn, place, -3, NB)
                if it.exists:
                    it.wait(pe, n1.hT_ready)
                    it.wait(pe, q_evacuated, back=2)
                    it.wait(pe, k_evacuated, back=2)
                    it.wait(pe, n1.evacuated, back=2)
                    for i in range(3):
                        for k in range(KT):
                            last = nc.tensor.matmul(bank[:, 2 + 3 * (it.r % 2) + i, :], hT[:, it.r % 2, k * P:(k + 1) * P],
                                                    w_qkv[:, k, i * D:(i + 1) * D], start=(k == 0), stop=(k == KT - 1))
                    last.then_inc(n1.projected, 1)

            run_steps(pe, NB, 1, 3, step1)
            pe.wait_ge(q_evacuated, NB)
            pe.wait_ge(k_evacuated, NB)
            pe.wait_ge(n1.evacuated, NB)

            def step2(turn, place):
                it = Item(turn, place, 1, NS)
                if it.exists:
                    b = slot_block(pe, it)
                    it.wait(pe, onehotT_ready)
                    it.wait(pe, product_ready, back=2)
                    for t in range(2):
                        last = nc.tensor.matmul(bank[:, 2 * (it.r % 2) + t, :], onehotT[:, it.r % 2, t, :],
                                                att[:, bass.ds((b + 1) * AW, D)], start=True, stop=True)
                    last.then_inc(queries_ready, 1)
                it = Item(turn, place, 2, NS)
                if it.exists:
                    it.wait(pe, onehot_ready)
                    it.wait(pe, onehotT_ready, back=2)
                    for t in range(2):
                        last = nc.tensor.transpose(bank[:, 6 + it.r % 2, t * P:(t + 1) * P], onehot[:, it.r, t, :],
                                                   ident[:, :])
                    last.then_inc(onehot_turned, 1)
                it = Item(turn, place, -1, NS)
                if it.exists:
                    it.wait(pe, message0_ready)
                    it.wait(pe, message1_ready)
                    it.wait(pe, att_added, back=1)
                    for t in range(2):
                        nc.tensor.matmul(bank[:, 4, :], onehot[:, it.r, t, :], message[:, it.r % 2, t, :],
                                         start=(t == 0), stop=(t == 1))
                    for t in range(2):
                        last = nc.tensor.matmul(bank[:, 5, 0:HEADS], onehot[:, it.r, t, :], weight[:, it.r % 2, t, :],
                                                start=(t == 0), stop=(t == 1))
                    last.then_inc(att_summed, 1)

            run_steps(pe, NS, 2, 1, step2)

            def row(it, k):
                return att[0:k, it.n * AW:it.n * AW + D] if it.fixed else att[0:k, bass.ds(it.n * AW, D)]

            def sum_rows(turn, place):
                it = Item(turn, place, 0, NB)
                k = TAIL if it.fixed and it.n == NB - 1 else P
                it.wait(pe, with_h)
                last = nc.tensor.matmul(bank[:, 0, :], ones[0:k, :], row(it, k), start=(it.fixed and it.n == 0),
                                        stop=(it.fixed and it.n == NB - 1))
                if it.fixed and it.n == NB - 1:
                    last.then_inc(mean_summed, 1)

            run_steps(pe, NB, 0, 0, sum_rows)

            def sum_squares(turn, place):
                it = Item(turn, place, 0, NB)
                k = TAIL if it.fixed and it.n == NB - 1 else P
                it.wait(pe, squared)
                last = nc.tensor.matmul(bank[:, 1, :], ones[0:k, :], square[0:k, it.r, :], start=(it.fixed and it.n == 0),
                                        stop=(it.fixed and it.n == NB - 1))
                last.then_inc(var_summed if it.fixed and it.n == NB - 1 else square_read, 1)

            run_steps(pe, NB, 0, 0, sum_squares)


_INS = ['x', 'src', 'dst', 'edge_weight', 'L0_gnn_W_gcn', 'L0_gnn_b_gcn', 'L0_gnn_W_fc', 'L0_gnn_b_fc',
        'L1_gnn_Wq', 'L1_gnn_Wk', 'L1_gnn_Wv', 'L1_gnn_bn_gamma', 'L1_gnn_bn_beta']


def kernel(**inputs):
    import numpy as _np
    import concourse.bacc as _bacc
    from concourse import mybir as _mybir
    from concourse.bass_utils import run_bass_kernel_spmd as _run

    nc = _bacc.Bacc("TRN2", target_bir_lowering=False, num_devices=1)
    arrays, args = {}, []
    for name in _INS:
        a = _np.ascontiguousarray(inputs[name])
        arrays[f"in_{name}_dram"] = a
        args.append(nc.dram_tensor(f"in_{name}_dram", a.shape, _mybir.dt.from_np(a.dtype), kind="ExternalInput").ap())
    shape = _np.shape(inputs['x'])
    args.append(nc.dram_tensor("out_0_dram", shape, _mybir.dt.float32, kind="ExternalOutput").ap())
    build_program(nc, *args)
    r = _run(nc, [arrays], core_ids=[0])
    return r.results[0]["out_0_dram"]
```

```python
import concourse.bass as bass
from concourse import mybir
from contextlib import ExitStack

P = 128
CHUNK = 2 * P
RING = 4
f32, i32 = mybir.dt.float32, mybir.dt.int32
ALU = mybir.AluOpType
ACT = mybir.ActivationFunctionType
AX = mybir.AxisListType
LN_EPS, BN_EPS, Z_EPS = 1e-5, 1e-5, 1e-6
CLIP = 5.0


def shifted(turn, place, by):
    return turn + (place + by) // RING, (place + by) % RING


def run_steps(engine, count, ahead, behind, step):
    first = -(-(behind + RING) // RING)
    last = max(first, (count - ahead) // RING)
    for s in range(-ahead, RING * first if last > first else count + behind):
        step(s // RING, s % RING)
    if last > first:
        with engine.Fori(first, last) as turn:
            for place in range(RING):
                step(turn, place)
        for s in range(RING * last, count + behind):
            step(s // RING, s % RING)


class Item:

    def __init__(self, turn, place, by, count):
        self.turn, self.r = shifted(turn, place, by)
        self.fixed = isinstance(self.turn, int)
        self.n = self.turn * RING + self.r
        self.exists = not self.fixed or 0 <= self.n < count

    def wait(self, engine, sem, back=0, per=1):
        if not self.fixed or self.n - back >= 0:
            engine.wait_ge(sem, (self.n + (1 - back)) * per)

    def wait_ring(self, engine, sems, per, back=0):
        if not self.fixed or self.turn - back >= 0:
            engine.wait_ge(sems[self.r], (self.turn + (1 - back)) * per)


def build_program(nc, x, src, dst, edge_weight, W_gcn, b_gcn, W_fc, b_fc, Wq, Wk, Wv, gamma, beta, out):
    N, D = x.shape
    E = src.shape[0]
    HID = W_gcn.shape[1]
    HEADS = 8
    DH = D // HEADS
    KT = D // P
    NB = -(-N // P)
    TAIL = N - (NB - 1) * P
    NC = -(-E // CHUNK)
    NG = -(-NC // P)
    NS = NC + NB - 1
    AW = D + HEADS
    HALF = AW // 2
    COLUMNS = 8
    NONE = NB * P
    assert (NONE + 1) * CHUNK < 1 << 24 and NG * P * CHUNK < 1 << 24
    assert HID == P and NS <= 512 and D == 512

    ctx = ExitStack()
    with ctx:
        def sb(name, shape, dt=f32):
            return ctx.enter_context(nc.sbuf_tensor(name, shape, dt))

        def sem(name):
            return ctx.enter_context(nc.semaphore(name))

        def dram(name, shape):
            return nc.dram_tensor(name, shape, f32, kind="Internal").ap()

        xg_dram = dram("xg_rows", (NB * P, HID))
        kv_dram = dram("kv_rows", (NB * P, 2 * D))
        x1_dram = dram("x1_rows", (NB * P, D))
        h1_dram = dram("h1_rows", (NB * P, D))
        dst_padded = nc.dram_tensor("dst_padded", (NG * P, CHUNK), i32, kind="Internal").ap()
        ordered = [nc.dram_tensor(f"ordered_{n}", (NG * P * CHUNK, 1), i32, kind="Internal").ap()
                   for n in ("dst", "src", "weight")]

        att = sb("att", [P, (NB + 1) * AW])
        rows_of = sb("rows_of", [P, NS, 2], i32)
        dst_in_block = sb("dst_in_block", [P, NS, 2])
        weight_of = sb("weight_of", [P, NS, 2])
        row_number = sb("row_number", [P, 1])
        out_of_order = sb("out_of_order", [1, 1], i32)
        same_block = sb("same_block", [P, NS])
        block_of = sb("block_of", [1, NS], i32)
        column = sb("column", [P, P])
        ident = sb("ident", [P, P])
        ones = sb("ones", [P, P])
        gather_rows = sb("gather_rows", [P, RING, 2], i32)
        mean_var = sb("mean_var", [P, RING, 2])
        stats = sb("stats", [P, RING, 6])
        spread = sb("spread", [P, RING])
        scale = sb("scale", [P, RING])
        shift = sb("shift", [P, RING])
        eps_col = sb("eps_col", [P, 1])

        AGG = NB * P
        ARENA = AGG + KT * 3 * D + 2 * D + 2 * RING * D + 2 * D + 2 * 2 * D + RING * P + D
        arena = sb("arena", [P, ARENA])

        class Carver:
            def __init__(self, at=0):
                self.at = at

            def take(self, *shape):
                n = 1
                for s in shape:
                    n *= s
                assert self.at + n <= ARENA, "arena"
                v = arena[:, self.at:self.at + n]
                self.at += n
                if len(shape) == 2:
                    v = v.rearrange("p (a b) -> p a b", a=shape[0])
                if len(shape) == 3:
                    v = v.rearrange("p (a b c) -> p a b c", a=shape[0], b=shape[1])
                return v

        c = Carver()
        aggT = c.take(AGG)
        w_qkv = c.take(KT, 3 * D)
        w_fcT = c.take(D)
        bias_fc = c.take(D)
        xt = c.take(RING, D)
        ht = c.take(RING, D)
        hT = c.take(2, D)
        shared_at = c.at
        kv_out = c.take(2, 2 * D)
        hidden = c.take(RING, P)
        c = Carver(shared_at)
        xg_out = c.take(RING, HID)
        xg_in = c.take(RING, 2, HID)
        onehot_w = c.take(RING, 2, P)
        c = Carver(AGG)
        w_gcn = sb("w_gcn", [P, KT, HID])
        b_gcn_col = sb("b_gcn_col", [P, 1])
        w_fc_rows = c.take(KT, HID)

        c = Carver()
        kv_in = c.take(RING, 2, 2 * D)
        onehot = c.take(RING, 2, P)
        onehotT = c.take(2, 2, P)
        message_at = c.take(RING, 2, AW)
        message = message_at.rearrange("p r t (h w) -> p r t h w", h=HEADS)
        product = c.take(2, 2, D)
        score = c.take(2, 2, HEADS)

        c = Carver()
        x1_in = c.take(RING, D)
        h1_in = c.take(RING, D)
        square = c.take(RING, D)
        recip_z = c.take(NB, HEADS)
        mean_b = c.take(D)
        scale_b = c.take(D)
        gamma_b = c.take(D)
        beta_b = c.take(D)

        class TableCarver(Carver):
            def take(self, *shape, dt=f32):
                n = 1
                for s in shape:
                    n *= s
                v = att[:, self.at:self.at + n]
                self.at += n
                if dt != f32:
                    v = v.bitcast(dt)
                if len(shape) == 2:
                    v = v.rearrange("p (a b) -> p a b", a=shape[0])
                return v

        c = TableCarver()
        dst_raw = c.take(NG, CHUNK, dt=i32)
        src_raw = c.take(NG, CHUNK, dt=i32)
        dst_rows = c.take(NG, CHUNK)
        src_rows = c.take(NG, CHUNK)
        w_rows = c.take(NG, CHUNK)
        slot_no = c.take(NS)
        chunk_of = c.take(NS)
        block_f = c.take(NS)
        block_base = c.take(NS)
        chunk_no = c.take(NG)
        chunk_end = c.take(NG)
        block_start = c.take(NB - 1)
        passed = c.take(NG, NB - 1)
        blocks_passed = c.take(NG)
        later = c.take(NG, NS)
        selects = c.take(NG, NS)
        partition_no = c.take(1)
        next_raw = c.take(NG, CHUNK, dt=i32)
        falls = c.take(NG, CHUNK)
        fall_count = c.take(1)
        rank = c.take(NG, CHUNK)
        rank_int = c.take(NG, CHUNK, dt=i32)
        threshold = c.take(NG, CHUNK)
        smaller = c.take(NG, CHUNK)
        own_offset = c.take(NG, CHUNK)
        edge_in_chunk = c.take(1, CHUNK)
        row_raw = c.take(CHUNK, dt=i32)
        row_key = c.take(CHUNK)
        compared = c.take(COLUMNS, CHUNK)
        is_own = c.take(NG)
        is_later = c.take(NG)
        staged = [c.take(1, dt=i32) for _ in range(4)]
        assert c.at <= (NB + 1) * AW

        bank = ctx.enter_context(nc.psum_tensor("bank", [P, 8, 512], f32))
        wide = bank[:, :, :].rearrange("p a b -> p (a b)")

        edges_in = sem("edges_in")
        order_counted = sem("order_counted")
        order_summed = sem("order_summed")
        order_known = sem("order_known")
        dst_stored = sem("dst_stored")
        row_in = sem("row_in")
        row_read = sem("row_read")
        ranked = sem("ranked")
        column_staged = sem("column_staged")
        column_out = [sem(f"column_out{n}") for n in range(3)]
        reordered = sem("reordered")
        edges_final = sem("edges_final")
        weights_in = sem("weights_in")
        padded = sem("padded")
        iotas = sem("iotas")
        vec = sem("vec")
        consts_ready = sem("consts_ready")
        later_ready = sem("later_ready")
        chunk_counted = sem("chunk_counted")
        selects_ready = sem("selects_ready")
        tables_in_psum = sem("tables_in_psum")
        tables_ready = sem("tables_ready")
        fcT_in_psum = sem("fcT_in_psum")
        fcT_ready = sem("fcT_ready")
        w_qkv_in = sem("w_qkv_in")
        act_go = sem("act_go")
        pool_go = sem("pool_go")
        sp_go = sem("sp_go")
        vec_go = sem("vec_go")

        class NodeSems:
            def __init__(self, tag):
                self.x_in = [sem(f"{tag}_x_in{r}") for r in range(RING)]
                self.stats_done = sem(f"{tag}_stats_done")
                self.aggr_done = sem(f"{tag}_aggr_done")
                self.var_ready = sem(f"{tag}_var_ready")
                self.std_ready = sem(f"{tag}_std_ready")
                self.scale_ready = sem(f"{tag}_scale_ready")
                self.norm_ready = sem(f"{tag}_norm_ready")
                self.h_ready = sem(f"{tag}_h_ready")
                self.turned = sem(f"{tag}_turned")
                self.hT_ready = sem(f"{tag}_hT_ready")
                self.projected = sem(f"{tag}_projected")
                self.evacuated = sem(f"{tag}_evacuated")
                self.stored = [sem(f"{tag}_stored{r}") for r in range(RING)]

        n0, n1 = NodeSems("n0"), NodeSems("n1")
        hidden_ready = sem("hidden_ready")
        fc_done = sem("fc_done")
        x_biased = sem("x_biased")
        x1_ready = sem("x1_ready")
        q_evacuated = sem("q_evacuated")
        k_evacuated = sem("k_evacuated")
        rows_stored = [sem(f"rows_stored{r}") for r in range(RING)]
        att_cleared = sem("att_cleared")

        index_ready = sem("index_ready")
        xg_gathered = [sem(f"xg_gathered{r}") for r in range(RING)]
        onehot_w_ready = sem("onehot_w_ready")
        summed = sem("summed")
        added = sem("added")

        index2_ready = sem("index2_ready")
        kv_gathered = [sem(f"kv_gathered{r}") for r in range(RING)]
        onehot_ready = sem("onehot_ready")
        onehot_turned = sem("onehot_turned")
        onehotT_ready = sem("onehotT_ready")
        queries_ready = sem("queries_ready")
        product_ready = sem("product_ready")
        score_ready = sem("score_ready")
        clipped = sem("clipped")
        weight_ready = sem("weight_ready")
        message0_ready = sem("message0_ready")
        message1_ready = sem("message1_ready")
        att_summed = sem("att_summed")
        att_added = sem("att_added")

        norm_in = sem("norm_in")
        z_ready = sem("z_ready")
        h1_back = [sem(f"h1_back{r}") for r in range(RING)]
        x1_back = [sem(f"x1_back{r}") for r in range(RING)]
        attended = sem("attended")
        with_h = sem("with_h")
        mean_summed = sem("mean_summed")
        mean_ready = sem("mean_ready")
        centered = sem("centered")
        squared = sem("squared")
        square_read = sem("square_read")
        var_summed = sem("var_summed")
        bn_var_ready = sem("bn_var_ready")
        bn_std_ready = sem("bn_std_ready")
        x1_biased = sem("x1_biased")
        scaled = sem("scaled")
        y_ready = sem("y_ready")
        y_stored = [sem(f"y_stored{r}") for r in range(RING)]

        block = ctx.enter_context(nc.Block())

        def load_chunks(engine, to, frm, length):
            full = length // CHUNK
            groups = full // P
            rest = full - groups * P
            odd = length - full * CHUNK
            if groups:
                engine.dma_start(to[:, 0:groups, :], frm[0:groups * P * CHUNK].rearrange(
                    "(g p k) -> p g k", g=groups, p=P)).then_inc(edges_in, 16)
            if rest:
                engine.dma_start(to[0:rest, groups, :], frm[groups * P * CHUNK:full * CHUNK].rearrange(
                    "(p k) -> p k", k=CHUNK)).then_inc(edges_in, 16)
            if odd:
                engine.dma_start(to[rest:rest + 1, groups, 0:odd],
                                 frm[full * CHUNK:length].rearrange("(p k) -> p k", p=1)).then_inc(edges_in, 16)
            return (groups > 0) + (rest > 0) + (odd > 0)

        loads = []

        def node_rows(t, n):
            if isinstance(n, int):
                return t[n * P:min(N, (n + 1) * P), :] if t is x or t is out else t[n * P:(n + 1) * P, :]
            return t[bass.ds(n * P, P), :]

        def used(t, n, tile):
            if isinstance(n, int) and (t is x or t is out):
                return tile[0:min(P, N - n * P)]
            return tile

        def message_of(it, t):
            to = message[:, it.r, t, :, :]
            return (to[:, :, 0:DH], kv_in[:, it.r, t, D:2 * D].rearrange("p (h d) -> p h d", h=HEADS),
                    to[:, :, DH:DH + 1].broadcast_to([P, HEADS, DH]))

        def slot_column(table, it, t=None):
            flat = table[:, :, :].rearrange("p j t -> p (j t)")
            at, n = (it.n * 2, 2) if t is None else (it.n * 2 + t, 1)
            return flat[:, at:at + n] if it.fixed else flat[:, bass.ds(at, n)]

        def slot_scalar(table, it):
            return table[:, it.n:it.n + 1] if it.fixed else table[:, bass.ds(it.n, 1)]

        def slot_block(engine, it):
            at = block_of[0:1, it.n:it.n + 1] if it.fixed else block_of[0:1, bass.ds(it.n, 1)]
            return engine.value_load(at, min_val=0, max_val=NB - 1)

        @block.sync
        def _(sp):
            sp.wait_ge(padded, 4)
            loads.append(load_chunks(sp, dst_raw, dst, E) + load_chunks(sp, next_raw, dst[1:E], E - 1)
                         + load_chunks(sp, src_raw, src, E) + load_chunks(sp, w_rows, edge_weight, E))
            sp.dma_start(w_gcn[:, :, :], W_gcn.rearrange("(k p) n -> p k n", p=P)).then_inc(weights_in, 16)
            sp.dma_start(w_fc_rows, W_fc.rearrange("(k p) n -> p k n", p=P)).then_inc(weights_in, 16)
            sp.dma_start(b_gcn_col[:, :], b_gcn.rearrange("(p a) -> p a", a=1)).then_inc(weights_in, 16)
            sp.dma_start(bias_fc, b_fc.rearrange("(a n) -> a n", a=1).broadcast_to([P, D])).then_inc(weights_in, 16)

            def step0(turn, place):
                it = Item(turn, place, 2, NB)
                if it.exists:
                    it.wait(sp, n0.h_ready, back=RING)
                    sp.sem_inc(sp_go, 1)
                    sp.dma_start(used(x, it.n, xt[:, it.r, :]), node_rows(x, it.n)).then_inc(n0.x_in[it.r], 16)
                it = Item(turn, place, -4, NB)
                if it.exists:
                    it.wait(sp, n0.evacuated)
                    sp.sem_inc(sp_go, 1)
                    sp.dma_start(node_rows(xg_dram, it.n), xg_out[:, it.r, :]).then_inc(n0.stored[it.r], 16)

            run_steps(sp, NB, 2, 4, step0)

            sp.wait_ge(fcT_in_psum, 1)
            for i, w in enumerate((Wq, Wk, Wv)):
                sp.dma_start(w_qkv[:, :, i * D:(i + 1) * D],
                             w.rearrange("(k p) n -> p k n", p=P)).then_inc(w_qkv_in, 16)

            def step1(turn, place):
                it = Item(turn, place, 2, NB)
                if it.exists:
                    it.wait_ring(sp, rows_stored, 32, back=1)
                    sp.sem_inc(sp_go, 1)
                    it.wait(sp, n1.h_ready, back=RING)
                    sp.sem_inc(sp_go, 1)
                    sp.dma_start(used(x, it.n, xt[:, it.r, :]), node_rows(x, it.n)).then_inc(n1.x_in[it.r], 16)
                it = Item(turn, place, -1, NB)
                if it.exists:
                    it.wait(sp, n1.h_ready)
                    sp.sem_inc(sp_go, 1)
                    sp.dma_start(node_rows(x1_dram, it.n), xt[:, it.r, :]).then_inc(rows_stored[it.r], 16)
                    sp.dma_start(node_rows(h1_dram, it.n), ht[:, it.r, :]).then_inc(rows_stored[it.r], 16)
                it = Item(turn, place, -4, NB)
                if it.exists:
                    it.wait(sp, n1.evacuated)
                    sp.sem_inc(sp_go, 1)
                    it.wait(sp, k_evacuated)
                    sp.sem_inc(sp_go, 1)
                    sp.dma_start(node_rows(kv_dram, it.n), kv_out[:, it.r % 2, :]).then_inc(n1.stored[it.r], 16)

            sp.wait_ge(n0.h_ready, NB)
            run_steps(sp, NB, 2, 4, step1)

            sp.wait_ge(att_added, NS)
            for r in range(RING):
                sp.wait_ge(rows_stored[r], 32 * len(range(r, NB, RING)))
            sp.dma_start(gamma_b, gamma.rearrange("(a n) -> a n", a=1).broadcast_to([P, D])).then_inc(norm_in, 16)
            sp.dma_start(beta_b, beta.rearrange("(a n) -> a n", a=1).broadcast_to([P, D])).then_inc(norm_in, 16)

            def step_h(turn, place):
                it = Item(turn, place, 2, NB)
                if it.exists:
                    it.wait(sp, with_h, back=RING)
                    sp.sem_inc(sp_go, 1)
                    sp.dma_start(h1_in[:, it.r, :], node_rows(h1_dram, it.n)).then_inc(h1_back[it.r], 16)

            run_steps(sp, NB, 2, 0, step_h)

            def step_y(turn, place):
                it = Item(turn, place, 2, NB)
                if it.exists:
                    it.wait_ring(sp, y_stored, 16, back=1)
                    sp.sem_inc(sp_go, 1)
                    sp.dma_start(x1_in[:, it.r, :], node_rows(x1_dram, it.n)).then_inc(x1_back[it.r], 16)
                it = Item(turn, place, -1, NB)
                if it.exists:
                    it.wait(sp, y_ready)
                    sp.sem_inc(sp_go, 1)
                    sp.dma_start(node_rows(out, it.n), used(out, it.n, x1_in[:, it.r, :])).then_inc(y_stored[it.r], 16)

            run_steps(sp, NB, 2, 1, step_y)
            for r in range(RING):
                sp.wait_ge(y_stored[r], 16 * len(range(r, NB, RING)))

        @block.gpsimd
        def _(pool):
            nc.gpsimd.memset(dst_raw, NONE).then_inc(padded, 1)
            nc.gpsimd.memset(next_raw, NONE).then_inc(padded, 1)
            nc.gpsimd.memset(src_raw, 0).then_inc(padded, 1)
            nc.gpsimd.memset(w_rows, 0.0).then_inc(padded, 1)
            free = dict(allow_small_or_imprecise_dtypes=True)
            nc.gpsimd.iota(column[:, :], pattern=[[1, P]], base=0, channel_multiplier=0, **free).then_inc(iotas, 1)
            nc.gpsimd.iota(partition_no, pattern=[[0, 1]], base=0, channel_multiplier=1, **free).then_inc(iotas, 1)
            nc.gpsimd.iota(slot_no, pattern=[[1, NS]], base=0, channel_multiplier=0, **free).then_inc(iotas, 1)
            nc.gpsimd.iota(chunk_no, pattern=[[P, NG]], base=0, channel_multiplier=1, **free).then_inc(iotas, 1)
            nc.gpsimd.iota(block_start, pattern=[[P, NB - 1]], base=P, channel_multiplier=0, **free).then_inc(iotas, 1)

            nc.gpsimd.iota(edge_in_chunk, pattern=[[0, 1], [1, CHUNK]], base=0, channel_multiplier=0,
                           **free).then_inc(iotas, 1)

            pool.wait_ge(order_known, 1)
            pool.wait_ge(edges_in, 16 * loads[0])
            unsorted = pool.value_load(out_of_order[0:1, 0:1], min_val=0, max_val=1)
            with pool.If(unsorted > 0):
                pool.dma_start(dst_padded.rearrange("(g p) k -> p g k", p=P), dst_raw).then_inc(dst_stored, 16)
                pool.wait_ge(dst_stored, 16)
                with pool.Fori(0, NG * P) as row:
                    pool.wait_ge(row_read, row + 1)
                    pool.sem_inc(pool_go, 1)
                    pool.dma_start(row_raw, dst_padded[bass.ds(row, 1), :].broadcast_to([P, CHUNK])).then_inc(row_in, 16)
                pool.wait_ge(ranked, 1)
                with pool.Fori(0, NG * CHUNK) as col:
                    for to, frm in zip(staged, (rank_int, dst_raw, src_raw, w_rows.bitcast(i32))):
                        last = nc.gpsimd.tensor_copy(to, frm.rearrange("p g k -> p (g k)")[:, bass.ds(col, 1)])
                    last.then_inc(column_staged, 1)
                    pool.wait_ge(column_staged, col + 1)
                    pool.sem_inc(pool_go, 1)
                    for to, frm, out_sem in zip(ordered, staged[1:], column_out):
                        pool.indirect_dma_start(out=to, out_offset=bass.IndirectOffsetOnAxis(ap=staged[0], axis=0),
                                                in_=frm, in_offset=None).then_inc(out_sem, 16)
                    for out_sem in column_out:
                        pool.wait_ge(out_sem, col * 16 + 16)
                        pool.sem_inc(pool_go, 1)
                for to, frm in zip((dst_raw, src_raw, w_rows.bitcast(i32)), ordered):
                    pool.dma_start(to, frm.rearrange("(g p k) a -> p g (k a)", g=NG, p=P)).then_inc(reordered, 16)
                pool.wait_ge(reordered, 48)
            pool.sem_inc(edges_final, 1)

            for r in range(RING):
                pool.wait_ge(n0.stored[r], 16 * len(range(r, NB, RING)))

            def gather0(turn, place):
                it = Item(turn, place, 0, NS)
                it.wait(pool, index_ready)
                it.wait(pool, summed, back=RING)
                pool.sem_inc(pool_go, 1)
                for t in range(2):
                    pool.indirect_dma_start(
                        out=xg_in[:, it.r, t, :], out_offset=None, in_=xg_dram,
                        in_offset=bass.IndirectOffsetOnAxis(ap=gather_rows[:, it.r, t:t + 1], axis=0),
                    ).then_inc(xg_gathered[it.r], 16)

            run_steps(pool, NS, 0, 0, gather0)

            pool.wait_ge(weights_in, 64)

            def bias(turn, place):
                it = Item(turn, place, 1, NB)
                if it.exists:
                    it.wait_ring(pool, n1.x_in, 16)
                    nc.gpsimd.tensor_tensor(xt[:, it.r, :], xt[:, it.r, :], bias_fc, ALU.add).then_inc(x_biased, 1)

            run_steps(pool, NB, 1, 0, bias)

            for r in range(RING):
                pool.wait_ge(n1.stored[r], 16 * len(range(r, NB, RING)))
                pool.wait_ge(rows_stored[r], 32 * len(range(r, NB, RING)))

            def gather_kv(it, t):
                pool.indirect_dma_start(
                    out=kv_in[:, it.r, t, :], out_offset=None, in_=kv_dram,
                    in_offset=bass.IndirectOffsetOnAxis(ap=gather_rows[:, it.r, t:t + 1], axis=0),
                ).then_inc(kv_gathered[it.r], 16)

            def step2(turn, place):
                ahead = Item(turn, place, 3, NS)
                if ahead.exists:
                    ahead.wait(pool, index2_ready)
                    ahead.wait(pool, message1_ready, back=RING)
                    ahead.wait(pool, message0_ready, back=RING)
                    pool.sem_inc(pool_go, 1)
                    gather_kv(ahead, 0)
                it = Item(turn, place, 0, NS)
                if it.exists:
                    it.wait(pool, score_ready)
                    pool.sem_inc(pool_go, 1)
                    flat = score[:, it.r % 2, :, :]
                    limit = CLIP * DH ** 0.5
                    nc.gpsimd.tensor_scalar(flat, flat, limit, -limit, ALU.min, ALU.max).then_inc(clipped, 1)
                if ahead.exists:
                    gather_kv(ahead, 1)
                if it.exists:
                    it.wait(pool, weight_ready)
                    it.wait(pool, att_summed, back=RING)
                    nc.gpsimd.tensor_tensor(*message_of(it, 0), ALU.mult).then_inc(message0_ready, 1)

            run_steps(pool, NS, 3, 0, step2)

            pool.wait_ge(norm_in, 32)

            def bias2(turn, place):
                it = Item(turn, place, 1, NB)
                if it.exists:
                    it.wait_ring(pool, x1_back, 16)
                    nc.gpsimd.tensor_tensor(x1_in[:, it.r, :], x1_in[:, it.r, :], beta_b, ALU.add).then_inc(x1_biased, 1)

            run_steps(pool, NB, 1, 0, bias2)

        def node_act(act, s, turn, place):
            it = Item(turn, place, 0, NB)
            if it.exists:
                it.wait(act, s.var_ready)
                nc.scalar.activation(scale[:, it.r:it.r + 1], spread[:, it.r:it.r + 1], ACT.Sqrt).then_inc(s.std_ready, 1)
            it = Item(turn, place, -1, NB)
            if it.exists:
                it.wait(act, s.norm_ready)
                it.wait(act, s.turned, back=RING)
                if s is n1:
                    it.wait_ring(act, rows_stored, 32, back=1)
                nc.scalar.activation(ht[:, it.r, :], xt[:, it.r, :], ACT.Relu, bias=shift[:, it.r:it.r + 1],
                                     scale=scale[:, it.r:it.r + 1]).then_inc(s.h_ready, 1)
            it = Item(turn, place, -2, NB)
            if it.exists:
                it.wait(act, s.turned)
                it.wait(act, s.projected, back=2)
                nc.scalar.activation(hT[:, it.r % 2, :], bank[:, it.r % 2 if s is n0 else 1, :],
                                     ACT.Copy).then_inc(s.hT_ready, 1)

        @block.scalar
        def _(act):
            run_steps(act, NB, 0, 2, lambda turn, place: node_act(act, n0, turn, place))

            act.wait_ge(tables_ready, 1)

            def index0(turn, place):
                it = Item(turn, place, 0, NS)
                it.wait_ring(act, xg_gathered, 32, back=1)
                act.sem_inc(act_go, 1)
                nc.scalar.activation(gather_rows[:, it.r, :], slot_column(rows_of, it), ACT.Copy).then_inc(index_ready, 1)

            run_steps(act, NS, 0, 0, index0)

            act.wait_ge(added, NS)
            act.wait_ge(weights_in, 64)

            def step1(turn, place):
                it = Item(turn, place, 1, NB)
                if it.exists:
                    it.wait(act, fc_done, back=RING)
                    act.sem_inc(act_go, 1)
                    nc.scalar.activation(hidden[:, it.r, :], aggT[:, it.n * P:(it.n + 1) * P] if it.fixed
                                         else aggT[:, bass.ds(it.n * P, P)], ACT.Identity,
                                         bias=b_gcn_col[:, :]).then_inc(hidden_ready, 1)
                node_act(act, n1, turn, place)
                it = Item(turn, place, -4, NB)
                if it.exists:
                    it.wait(act, n1.projected)
                    act.sem_inc(act_go, 1)
                    at = (it.n + 1) * AW
                    nc.scalar.activation(att[:, at:at + D] if it.fixed else att[:, bass.ds(at, D)],
                                         bank[:, 2 + 3 * (it.r % 2), :], ACT.Copy).then_inc(q_evacuated, 1)
                    if not it.fixed or it.n >= 2:
                        two = Item(turn, place, -6, NB)
                        two.wait_ring(act, n1.stored, 16)
                    nc.scalar.activation(kv_out[:, it.r % 2, 0:D], bank[:, 3 + 3 * (it.r % 2), :],
                                         ACT.Copy).then_inc(k_evacuated, 1)

            run_steps(act, NB, 1, 4, step1)

            for r in range(RING):
                act.wait_ge(n1.stored[r], 16 * len(range(r, NB, RING)))
                act.wait_ge(rows_stored[r], 32 * len(range(r, NB, RING)))

            def step2(turn, place):
                it = Item(turn, place, 4, NS)
                if it.exists:
                    it.wait_ring(act, kv_gathered, 32, back=1)
                    act.sem_inc(act_go, 1)
                    nc.scalar.activation(gather_rows[:, it.r, :], slot_column(rows_of, it),
                                         ACT.Copy).then_inc(index2_ready, 1)
                it = Item(turn, place, 1, NS)
                if it.exists:
                    it.wait(act, onehot_turned)
                    it.wait(act, queries_ready, back=2)
                    nc.scalar.activation(onehotT[:, it.r % 2, :, :], bank[:, 6 + it.r % 2, 0:CHUNK].rearrange(
                        "p (t e) -> p t e", t=2), ACT.Copy).then_inc(onehotT_ready, 1)
                it = Item(turn, place, 0, NS)
                if it.exists:
                    it.wait(act, clipped)
                    it.wait(act, att_summed, back=RING)
                    nc.scalar.activation(message[:, it.r, :, :, DH], score[:, it.r % 2, :, :], ACT.Exp,
                                         scale=DH ** -0.5).then_inc(weight_ready, 1)
                    it.wait(act, weight_ready)
                    for h in range(HEADS):
                        last = nc.scalar.activation(message[:, it.r, 1, h, 0:DH],
                                                    kv_in[:, it.r, 1, D + h * DH:D + (h + 1) * DH], ACT.Copy,
                                                    scale=message[:, it.r, 1, h, DH:DH + 1])
                    last.then_inc(message1_ready, 1)

            run_steps(act, NS, 4, 0, step2)

            def squares(turn, place):
                it = Item(turn, place, 0, NB)
                it.wait(act, centered)
                it.wait(act, square_read, back=RING)
                act.sem_inc(act_go, 1)
                at = it.n * AW
                nc.scalar.activation(square[:, it.r, :], att[:, at:at + D] if it.fixed else att[:, bass.ds(at, D)],
                                     ACT.Square).then_inc(squared, 1)

            run_steps(act, NB, 0, 0, squares)
            act.wait_ge(bn_var_ready, 1)
            nc.scalar.activation(scale_b, scale_b, ACT.Sqrt).then_inc(bn_std_ready, 1)

        def rank_edges(dve):
            flat = lambda t: t.rearrange("p g k -> p (g k)")
            nc.vector.memset(rank, 0.0)
            nc.vector.tensor_copy(dst_rows, dst_raw)
            dve.drain()
            dve.sem_inc(row_read, 1)
            with dve.Fori(0, NG * P) as row:
                dve.wait_ge(row_in, row * 16 + 16)
                nc.vector.tensor_copy(row_key, row_raw)
                dve.drain()
                dve.sem_inc(row_read, 1)
                nc.vector.tensor_scalar(row_key, row_key, float(CHUNK), None, ALU.mult)
                dve.drain()
                nc.vector.tensor_tensor(row_key, row_key, edge_in_chunk[:, 0, :], ALU.add)
                nc.vector.tensor_scalar(is_own, chunk_no, row_number[:, 0:1], None, ALU.is_equal)
                nc.vector.tensor_scalar(is_later, chunk_no, row_number[:, 0:1], float(CHUNK), ALU.is_gt, ALU.mult)
                nc.vector.tensor_scalar(threshold, dst_rows, float(CHUNK), None, ALU.mult)
                dve.drain()
                for g in range(NG):
                    nc.vector.tensor_scalar(own_offset[:, g, :], edge_in_chunk[:, 0, :], is_own[:, g:g + 1],
                                            is_later[:, g:g + 1], ALU.mult, ALU.add)
                nc.vector.tensor_scalar(row_number[:, :], row_number[:, :], 1.0, None, ALU.add)
                dve.drain()
                nc.vector.tensor_tensor(threshold, threshold, own_offset, ALU.add)
                dve.drain()
                with dve.Fori(0, NG * CHUNK // COLUMNS) as group:
                    nc.vector.tensor_tensor(compared, row_key.unsqueeze(1).broadcast_to([P, COLUMNS, CHUNK]),
                                            flat(threshold)[:, bass.ds(group * COLUMNS, COLUMNS)].unsqueeze(2).broadcast_to(
                                                [P, COLUMNS, CHUNK]), ALU.is_lt)
                    dve.drain()
                    nc.vector.tensor_reduce(flat(smaller)[:, bass.ds(group * COLUMNS, COLUMNS)], compared, AX.X, ALU.add)
                    dve.drain()
                nc.vector.tensor_tensor(rank, rank, smaller, ALU.add)
                dve.drain()
            nc.vector.tensor_copy(rank_int, rank)
            dve.drain()
            dve.sem_inc(ranked, 1)

        @block.vector
        def _(dve):
            steps = [0]

            def link(instruction):
                steps[0] += 1
                instruction.then_inc(vec, 1)
                dve.wait_ge(vec, steps[0])

            nc.vector.memset(ones[:, :], 1.0)
            nc.vector.memset(row_number[:, :], 0.0)
            link(nc.vector.memset(aggT, 0.0))
            dve.wait_ge(iotas, 6)
            nc.vector.tensor_scalar(ident[:, :], column[:, :], partition_no, None, ALU.is_equal).then_inc(consts_ready, 1)

            dve.wait_ge(edges_in, 16 * loads[0])
            nc.vector.tensor_tensor(falls, next_raw, dst_raw, ALU.is_lt).then_inc(order_counted, 1)
            dve.wait_ge(order_counted, 1)
            nc.vector.tensor_reduce(fall_count, falls.rearrange("p g k -> p (g k)"), AX.X, ALU.add).then_inc(order_counted, 1)
            dve.wait_ge(order_summed, 1)
            link(nc.vector.tensor_scalar(out_of_order[:, :], bank[0:1, 0, 0:1], 1.0, None, ALU.min))
            dve.sem_inc(order_known, 1)
            unsorted = dve.value_load(out_of_order[0:1, 0:1], min_val=0, max_val=1)
            with dve.If(unsorted > 0):
                rank_edges(dve)
            dve.wait_ge(edges_final, 1)
            nc.vector.tensor_copy(src_rows, src_raw)
            link(nc.vector.tensor_copy(dst_rows, dst_raw))
            last_dst = dst_rows[:, :, CHUNK - 1:CHUNK]
            link(nc.vector.tensor_tensor(passed, last_dst.broadcast_to([P, NG, NB - 1]),
                                         block_start.unsqueeze(1).broadcast_to([P, NG, NB - 1]), ALU.is_ge))
            link(nc.vector.tensor_reduce(blocks_passed, passed, AX.X, ALU.add))
            link(nc.vector.tensor_tensor(chunk_end, blocks_passed, chunk_no, ALU.add))
            for g in range(NG):
                last = nc.vector.tensor_scalar(later[:, g, :], slot_no, chunk_end[:, g:g + 1], None, ALU.is_gt)
            last.then_inc(later_ready, 1)
            dve.wait_ge(chunk_counted, 1)
            link(nc.vector.tensor_copy(chunk_of, bank[:, 0, 0:NS]))
            for g in range(NG):
                last = nc.vector.tensor_scalar(selects[:, g, :], chunk_of, chunk_no[:, g:g + 1], None, ALU.is_equal)
            last.then_inc(selects_ready, 1)
            link(nc.vector.tensor_tensor(block_f, slot_no, chunk_of, ALU.subtract))
            nc.vector.tensor_scalar(block_base, block_f, float(P), None, ALU.mult)
            nc.vector.tensor_copy(block_of[:, :], block_f[0:1, :])
            nc.vector.memset(same_block[:, 0:1], 0.0)
            link(nc.vector.tensor_tensor(same_block[:, 1:NS], block_f[:, 1:NS], block_f[:, 0:NS - 1], ALU.is_equal))
            dve.wait_ge(tables_in_psum, 1)
            for t in range(2):
                nc.vector.tensor_tensor(dst_in_block[:, :, t], bank[:, 1 + t, 0:NS], block_base, ALU.subtract)
                nc.vector.tensor_copy(rows_of[:, :, t], bank[:, 3 + t, 0:NS])
                last = nc.vector.tensor_copy(weight_of[:, :, t], bank[:, 5 + t, 0:NS])
            last.then_inc(tables_ready, 1)
            dve.wait_ge(tables_ready, 1)
            dve.wait_ge(fcT_in_psum, 1)
            nc.vector.tensor_copy(w_fcT, bank[:, 7, :]).then_inc(fcT_ready, 1)

            def node_stats(s, turn, place):
                it = Item(turn, place, 0, NB)
                if it.exists:
                    if s is n0:
                        it.wait_ring(dve, s.x_in, 16)
                    else:
                        it.wait(dve, x1_ready)
                    it.wait(dve, s.h_ready, back=RING)
                    nc.vector.bn_stats(stats[:, it.r, :], xt[:, it.r, :]).then_inc(s.stats_done, 1)
                    it.wait(dve, s.stats_done)
                    dve.sem_inc(vec_go, 1)
                    nc.vector.bn_aggr(mean_var[:, it.r, :], stats[:, it.r, :]).then_inc(s.aggr_done, 1)
                    it.wait(dve, s.aggr_done)
                    nc.vector.tensor_scalar(spread[:, it.r:it.r + 1], mean_var[:, it.r, 1:2], LN_EPS, None,
                                            ALU.add).then_inc(s.var_ready, 1)
                it = Item(turn, place, -1, NB)
                if it.exists:
                    it.wait(dve, s.std_ready)
                    nc.vector.reciprocal(scale[:, it.r:it.r + 1], scale[:, it.r:it.r + 1]).then_inc(s.scale_ready, 1)
                    it.wait(dve, s.scale_ready)
                    nc.vector.scalar_tensor_tensor(shift[:, it.r:it.r + 1], mean_var[:, it.r, 0:1], -1.0,
                                                   scale[:, it.r:it.r + 1], ALU.mult, ALU.mult).then_inc(s.norm_ready, 1)

            def step0(turn, place):
                node_stats(n0, turn, place)
                it = Item(turn, place, -3, NB)
                if it.exists:
                    it.wait(dve, n0.projected)
                    it.wait_ring(dve, n0.stored, 16, back=1)
                    nc.vector.tensor_copy(xg_out[:, it.r, :], bank[:, 2 + it.r % 2, 0:HID]).then_inc(n0.evacuated, 1)

            run_steps(dve, NB, 0, 3, step0)
            sums = att[:, :].rearrange("p (b w) -> p b w", w=AW)
            nc.vector.memset(sums[:, :, D:AW], 0.0)
            link(nc.vector.memset(sums[:, 0:1, 0:D], 0.0))

            for r in range(RING):
                dve.wait_ge(n0.stored[r], 16 * len(range(r, NB, RING)))

            def edges0(turn, place):
                it = Item(turn, place, 1, NS)
                if it.exists:
                    it.wait(dve, summed, back=RING)
                    for t in range(2):
                        last = nc.vector.tensor_scalar(onehot_w[:, it.r, t, :], column[:, :],
                                                       slot_column(dst_in_block, it, t), slot_column(weight_of, it, t),
                                                       ALU.is_equal, ALU.mult)
                    last.then_inc(onehot_w_ready, 1)
                it = Item(turn, place, -1, NS)
                if it.exists:
                    b = slot_block(dve, it)
                    it.wait(dve, summed)
                    it.wait(dve, added, back=1)
                    to = aggT[:, bass.ds(b * P, P)]
                    nc.vector.tensor_tensor(to, to, bank[:, it.r % 2, 0:P], ALU.add).then_inc(added, 1)

            run_steps(dve, NS, 1, 1, edges0)

            def step1(turn, place):
                it = Item(turn, place, 0, NB)
                if it.exists:
                    it.wait(dve, fc_done)
                    it.wait(dve, x_biased)
                    nc.vector.tensor_tensor(xt[:, it.r, :], xt[:, it.r, :], bank[:, 0, :], ALU.add).then_inc(x1_ready, 1)
                node_stats(n1, turn, place)
                it = Item(turn, place, -4, NB)
                if it.exists:
                    it.wait(dve, n1.projected)
                    if not it.fixed or it.n >= 2:
                        two = Item(turn, place, -6, NB)
                        two.wait_ring(dve, n1.stored, 16)
                    nc.vector.tensor_copy(kv_out[:, it.r % 2, D:2 * D],
                                          bank[:, 4 + 3 * (it.r % 2), :]).then_inc(n1.evacuated, 1)

            run_steps(dve, NB, 0, 4, step1)

            for r in range(RING):
                dve.wait_ge(n1.stored[r], 16 * len(range(r, NB, RING)))
                dve.wait_ge(rows_stored[r], 32 * len(range(r, NB, RING)))

            def step2(turn, place):
                b = None
                it = Item(turn, place, 0, NS)
                if it.exists:
                    it.wait(dve, weight_ready, back=2)
                    it.wait(dve, score_ready, back=2)
                    it.wait_ring(dve, kv_gathered, 32)
                    it.wait(dve, queries_ready)
                    nc.vector.tensor_tensor(product[:, it.r % 2, :, :], kv_in[:, it.r, :, 0:D], bank[:, 2 * (it.r % 2):2 * (it.r % 2) + 2, :],
                                            ALU.mult).then_inc(product_ready, 1)
                    it.wait(dve, product_ready)
                    nc.vector.tensor_reduce(score[:, it.r % 2, :, :].rearrange("p t h -> p (t h)"),
                                            product[:, it.r % 2, :, :].rearrange("p t (h d) -> p (t h) d", h=HEADS),
                                            AX.X, ALU.add).then_inc(score_ready, 1)
                    before = Item(turn, place, -2, NS)
                    b = slot_block(dve, before) if before.exists else None
                it = Item(turn, place, -2, NS)
                if it.exists:
                    if not Item(turn, place, 0, NS).exists:
                        b = slot_block(dve, it)
                    it.wait(dve, att_summed)
                    it.wait(dve, att_added, back=1)
                    to = att[:, bass.ds(b * AW, AW)].rearrange("p (a w) -> p a w", a=2)
                    nc.vector.scalar_tensor_tensor(to, to, slot_scalar(same_block, it), bank[:, 4:6, 0:HALF],
                                                   ALU.mult, ALU.add).then_inc(att_added, 1)
                it = Item(turn, place, 2, NS)
                if it.exists:
                    it.wait(dve, att_summed, back=RING)
                    for t in range(2):
                        last = nc.vector.tensor_scalar(onehot[:, it.r, t, :], column[:, :],
                                                       slot_column(dst_in_block, it, t), None, ALU.is_equal)
                    last.then_inc(onehot_ready, 1)

            run_steps(dve, NS, 2, 2, step2)

            dve.wait_ge(att_added, NS)
            z = att[:, 0:NB * AW].rearrange("p (b h w) -> p b h w", h=HEADS, w=DH + 1)[:, :, :, DH]
            link(nc.vector.tensor_scalar(recip_z, z, Z_EPS, None, ALU.add))
            link(nc.vector.reciprocal(recip_z, recip_z))
            flat_z = recip_z.rearrange("p b h -> p (b h)")

            def row(it):
                return att[:, it.n * AW:it.n * AW + D] if it.fixed else att[:, bass.ds(it.n * AW, D)]

            def attend(turn, place):
                it = Item(turn, place, 0, NB)
                v = att[:, it.n * AW:(it.n + 1) * AW] if it.fixed else att[:, bass.ds(it.n * AW, AW)]
                v = v.rearrange("p (h w) -> p h w", h=HEADS)[:, :, 0:DH]
                part = square[:, it.r, :]
                rz = flat_z[:, it.n * HEADS:(it.n + 1) * HEADS] if it.fixed else flat_z[:, bass.ds(it.n * HEADS, HEADS)]
                nc.vector.tensor_tensor(part.rearrange("p (h d) -> p h d", h=HEADS), v, rz.unsqueeze(2).broadcast_to([P, HEADS, DH]), ALU.mult).then_inc(attended, 1)
                it.wait_ring(dve, h1_back, 16)
                it.wait(dve, attended)
                nc.vector.tensor_tensor(row(it), part, h1_in[:, it.r, :], ALU.add).then_inc(with_h, 1)

            run_steps(dve, NB, 0, 0, attend)
            dve.wait_ge(mean_summed, 1)
            link(nc.vector.tensor_scalar(mean_b, bank[:, 0, :], 1.0 / N, None, ALU.mult))

            def center(turn, place):
                it = Item(turn, place, 0, NB)
                nc.vector.tensor_tensor(row(it), row(it), mean_b, ALU.subtract).then_inc(centered, 1)

            run_steps(dve, NB, 0, 0, center)
            dve.wait_ge(var_summed, 1)
            nc.vector.tensor_scalar(scale_b, bank[:, 1, :], 1.0 / N, BN_EPS, ALU.mult, ALU.add).then_inc(bn_var_ready, 1)
            dve.wait_ge(bn_std_ready, 1)
            link(nc.vector.reciprocal(scale_b, scale_b))
            dve.wait_ge(norm_in, 32)
            link(nc.vector.tensor_tensor(scale_b, scale_b, gamma_b, ALU.mult))

            def finish(turn, place):
                it = Item(turn, place, 0, NB)
                nc.vector.tensor_tensor(row(it), row(it), scale_b, ALU.mult).then_inc(scaled, 1)
                it.wait(dve, scaled)
                it.wait(dve, x1_biased)
                nc.vector.tensor_tensor(x1_in[:, it.r, :], row(it), x1_in[:, it.r, :], ALU.add).then_inc(y_ready, 1)

            run_steps(dve, NB, 0, 0, finish)

        @block.tensor
        def _(pe):
            def turn_rows(s, it, to):
                for k in range(KT):
                    last = nc.tensor.transpose(to[:, k * P:(k + 1) * P], ht[:, it.r, k * P:(k + 1) * P], ident[:, :])
                last.then_inc(s.turned, 1)

            pe.wait_ge(order_counted, 2)
            nc.tensor.matmul(bank[:, 0, 0:1], ones[:, :], fall_count, start=True, stop=True).then_inc(order_summed, 1)

            pe.wait_ge(later_ready, 1)
            for g in range(NG):
                last = nc.tensor.matmul(bank[:, 0, 0:NS], ones[:, :], later[:, g, :], start=(g == 0), stop=(g == NG - 1))
            last.then_inc(chunk_counted, 1)
            pe.wait_ge(selects_ready, 1)
            for a, rows in enumerate((dst_rows, src_rows, w_rows)):
                for t in range(2):
                    for g in range(NG):
                        last = nc.tensor.matmul(bank[:, 1 + 2 * a + t, 0:NS], rows[:, g, t * P:(t + 1) * P],
                                                selects[:, g, :], start=(g == 0), stop=(g == NG - 1))
            last.then_inc(tables_in_psum, 1)
            pe.wait_ge(weights_in, 64)
            for k in range(KT):
                last = nc.tensor.transpose(bank[:, 7, k * P:(k + 1) * P], w_fc_rows[:, k, :], ident[:, :])
            last.then_inc(fcT_in_psum, 1)
            pe.wait_ge(tables_ready, 1)

            def step0(turn, place):
                it = Item(turn, place, -1, NB)
                if it.exists:
                    it.wait(pe, n0.h_ready)
                    it.wait(pe, n0.hT_ready, back=2)
                    turn_rows(n0, it, bank[:, it.r % 2, :])
                it = Item(turn, place, -2, NB)
                if it.exists:
                    it.wait(pe, n0.hT_ready)
                    it.wait(pe, n0.evacuated, back=2)
                    for k in range(KT):
                        last = nc.tensor.matmul(bank[:, 2 + it.r % 2, 0:HID], hT[:, it.r % 2, k * P:(k + 1) * P],
                                                w_gcn[:, k, :], start=(k == 0), stop=(k == KT - 1))
                    last.then_inc(n0.projected, 1)

            run_steps(pe, NB, 0, 2, step0)

            def edges0(turn, place):
                it = Item(turn, place, 0, NS)
                it.wait_ring(pe, xg_gathered, 32)
                it.wait(pe, onehot_w_ready)
                it.wait(pe, added, back=2)
                for t in range(2):
                    last = nc.tensor.matmul(bank[:, it.r % 2, 0:P], xg_in[:, it.r, t, :], onehot_w[:, it.r, t, :],
                                            start=(t == 0), stop=(t == 1))
                last.then_inc(summed, 1)

            run_steps(pe, NS, 0, 0, edges0)
            pe.wait_ge(fcT_ready, 1)
            pe.wait_ge(w_qkv_in, 48)

            def step1(turn, place):
                it = Item(turn, place, 1, NB)
                if it.exists:
                    it.wait(pe, hidden_ready)
                    it.wait(pe, x1_ready, back=1)
                    nc.tensor.matmul(bank[:, 0, :], hidden[:, it.r, :], w_fcT, start=True, stop=True).then_inc(fc_done, 1)
                it = Item(turn, place, -2, NB)
                if it.exists:
                    it.wait(pe, n1.h_ready)
                    it.wait(pe, n1.hT_ready, back=1)
                    turn_rows(n1, it, bank[:, 1, :])
                it = Item(turn, place, -3, NB)
                if it.exists:
                    it.wait(pe, n1.hT_ready)
                    it.wait(pe, q_evacuated, back=2)
                    it.wait(pe, k_evacuated, back=2)
                    it.wait(pe, n1.evacuated, back=2)
                    for i in range(3):
                        for k in range(KT):
                            last = nc.tensor.matmul(bank[:, 2 + 3 * (it.r % 2) + i, :], hT[:, it.r % 2, k * P:(k + 1) * P],
                                                    w_qkv[:, k, i * D:(i + 1) * D], start=(k == 0), stop=(k == KT - 1))
                    last.then_inc(n1.projected, 1)

            run_steps(pe, NB, 1, 3, step1)
            pe.wait_ge(q_evacuated, NB)
            pe.wait_ge(k_evacuated, NB)
            pe.wait_ge(n1.evacuated, NB)

            def step2(turn, place):
                it = Item(turn, place, 1, NS)
                if it.exists:
                    it.wait(pe, onehot_ready)
                    it.wait(pe, onehotT_ready, back=2)
                    for t in range(2):
                        last = nc.tensor.transpose(bank[:, 6 + it.r % 2, t * P:(t + 1) * P], onehot[:, it.r, t, :],
                                                   ident[:, :])
                    last.then_inc(onehot_turned, 1)
                it = Item(turn, place, -2, NS)
                if it.exists:
                    it.wait(pe, message0_ready)
                    it.wait(pe, message1_ready)
                    it.wait(pe, att_added, back=1)
                    for half in range(2):
                        for t in range(2):
                            last = nc.tensor.matmul(bank[:, 4 + half, 0:HALF], onehot[:, it.r, t, :],
                                                    message_at[:, it.r, t, half * HALF:(half + 1) * HALF],
                                                    start=(t == 0), stop=(t == 1))
                    last.then_inc(att_summed, 1)
                it = Item(turn, place, 1, NS)
                if it.exists:
                    b = slot_block(pe, it)
                    it.wait(pe, onehotT_ready)
                    it.wait(pe, product_ready, back=2)
                    for t in range(2):
                        last = nc.tensor.matmul(bank[:, 2 * (it.r % 2) + t, :], onehotT[:, it.r % 2, t, :],
                                                att[:, bass.ds((b + 1) * AW, D)], start=True, stop=True)
                    last.then_inc(queries_ready, 1)

            run_steps(pe, NS, 1, 2, step2)

            def row(it, k):
                return att[0:k, it.n * AW:it.n * AW + D] if it.fixed else att[0:k, bass.ds(it.n * AW, D)]

            def sum_rows(turn, place):
                it = Item(turn, place, 0, NB)
                k = TAIL if it.fixed and it.n == NB - 1 else P
                it.wait(pe, with_h)
                last = nc.tensor.matmul(bank[:, 0, :], ones[0:k, :], row(it, k), start=(it.fixed and it.n == 0),
                                        stop=(it.fixed and it.n == NB - 1))
                if it.fixed and it.n == NB - 1:
                    last.then_inc(mean_summed, 1)

            run_steps(pe, NB, 0, 0, sum_rows)

            def sum_squares(turn, place):
                it = Item(turn, place, 0, NB)
                k = TAIL if it.fixed and it.n == NB - 1 else P
                it.wait(pe, squared)
                last = nc.tensor.matmul(bank[:, 1, :], ones[0:k, :], square[0:k, it.r, :], start=(it.fixed and it.n == 0),
                                        stop=(it.fixed and it.n == NB - 1))
                last.then_inc(var_summed if it.fixed and it.n == NB - 1 else square_read, 1)

            run_steps(pe, NB, 0, 0, sum_squares)


_INS = ['x', 'src', 'dst', 'edge_weight', 'L0_gnn_W_gcn', 'L0_gnn_b_gcn', 'L0_gnn_W_fc', 'L0_gnn_b_fc',
        'L1_gnn_Wq', 'L1_gnn_Wk', 'L1_gnn_Wv', 'L1_gnn_bn_gamma', 'L1_gnn_bn_beta']


def kernel(**inputs):
    import numpy as _np
    import concourse.bacc as _bacc
    from concourse import mybir as _mybir
    from concourse.bass_utils import run_bass_kernel_spmd as _run

    nc = _bacc.Bacc("TRN2", target_bir_lowering=False, num_devices=1)
    arrays, args = {}, []
    for name in _INS:
        a = _np.ascontiguousarray(inputs[name])
        arrays[f"in_{name}_dram"] = a
        args.append(nc.dram_tensor(f"in_{name}_dram", a.shape, _mybir.dt.from_np(a.dtype), kind="ExternalInput").ap())
    shape = _np.shape(inputs['x'])
    args.append(nc.dram_tensor("out_0_dram", shape, _mybir.dt.float32, kind="ExternalOutput").ap())
    build_program(nc, *args)
    r = _run(nc, [arrays], core_ids=[0])
    return r.results[0]["out_0_dram"]
```

```python
import concourse.bass as bass
from concourse import mybir
from contextlib import ExitStack

P = 128
CHUNK = 2 * P
RING = 4
LONG = 12
ROWS = 8
GROUP = 4
f32, i32 = mybir.dt.float32, mybir.dt.int32
ALU = mybir.AluOpType
ACT = mybir.ActivationFunctionType
AX = mybir.AxisListType
LN_EPS, BN_EPS, Z_EPS = 1e-5, 1e-5, 1e-6
CLIP = 5.0


def run_steps(engine, count, ahead, behind, step, ring=RING):
    first = -(-(behind + ring) // ring)
    last = max(first, (count - 1 - ahead) // ring)
    for s in range(-ahead, ring * first if last > first else count + behind):
        step(s // ring, s % ring)
    if last > first:
        with engine.Fori(first, last) as turn:
            for place in range(ring):
                step(turn, place)
        for s in range(ring * last, count + behind):
            step(s // ring, s % ring)


class Item:

    def __init__(self, turn, place, by, count, ring=RING):
        self.turn, self.r = turn + (place + by) // ring, (place + by) % ring
        self.fixed = isinstance(self.turn, int)
        self.n = self.turn * ring + self.r
        self.exists = not self.fixed or 0 <= self.n < count

    def wait(self, engine, sem, back=0, per=1):
        if not self.fixed or self.n - back >= 0:
            engine.wait_ge(sem, (self.n + (1 - back)) * per)

    def wait_ring(self, engine, sems, per, back=0):
        if not self.fixed or self.turn - back >= 0:
            engine.wait_ge(sems[self.r], (self.turn + (1 - back)) * per)


def build_program(nc, x, src, dst, edge_weight, W_gcn, b_gcn, W_fc, b_fc, Wq, Wk, Wv, gamma, beta, out):
    N, D = x.shape
    E = src.shape[0]
    HID = W_gcn.shape[1]
    HEADS = 8
    DH = D // HEADS
    KT = D // P
    NB = -(-N // P)
    TAIL = N - (NB - 1) * P
    NC = -(-E // CHUNK)
    NG = -(-NC // P)
    NS = NC + NB - 1
    MODULUS = 1 << NB.bit_length()
    COUNTS = 8
    assert COUNTS > GROUP
    assert MODULUS ** GROUP <= 1 << 24 and LONG % GROUP == 0
    AW = D + HEADS
    HALF = AW // 2
    COLUMNS = 8
    NONE = NB * P
    assert (NONE + 1) * CHUNK < 1 << 24 and NG * P * CHUNK < 1 << 24
    assert HID == P and NS <= 512 and D == 512

    ctx = ExitStack()
    with ctx:
        def sb(name, shape, dt=f32):
            return ctx.enter_context(nc.sbuf_tensor(name, shape, dt))

        def sem(name):
            return ctx.enter_context(nc.semaphore(name))

        def dram(name, shape):
            return nc.dram_tensor(name, shape, f32, kind="Internal").ap()

        xg_dram = dram("xg_rows", (NB * P, HID))
        kv_dram = dram("kv_rows", (NB * P, 2 * D))
        x1_dram = dram("x1_rows", (NB * P, D))
        h1_dram = dram("h1_rows", (NB * P, D))
        dst_padded = nc.dram_tensor("dst_padded", (NG * P, CHUNK), i32, kind="Internal").ap()
        ordered = [nc.dram_tensor(f"ordered_{n}", (NG * P * CHUNK, 1), i32, kind="Internal").ap()
                   for n in ("dst", "src", "weight")]

        att = sb("att", [P, (NB + 1) * AW])
        rows_of = sb("rows_of", [P, NS, 2], i32)
        dst_in_block = sb("dst_in_block", [P, NS, 2])
        weight_of = sb("weight_of", [P, NS, 2])
        row_number = sb("row_number", [P, 1])
        out_of_order = sb("out_of_order", [1, 1], i32)
        same_block = sb("same_block", [P, NS])
        block_of = sb("block_of", [1, NS], i32)
        finished = sb("finished", [1, NS], i32)
        group_ends = sb("group_ends", [1, NS], i32)
        column = sb("column", [P, P])
        ident = sb("ident", [P, P])
        ones = sb("ones", [P, P])
        gather_rows = sb("gather_rows", [P, LONG, 2], i32)
        mean_var = sb("mean_var", [P, RING, 2])
        stats = sb("stats", [P, RING, 6])
        spread = sb("spread", [P, RING])
        scale = sb("scale", [P, RING])
        shift = sb("shift", [P, RING])
        eps_col = sb("eps_col", [P, 1])

        ARENA = 2 * RING * 2 * D + RING * 2 * P + 2 * 2 * P + RING * 2 * AW + 2 * 2 * D + 2 * 2 * HEADS
        ARENA = max(ARENA + GROUP * P, KT * 3 * D + 8 * D + (4 * LONG + GROUP + 1) * P)
        arena = sb("arena", [P, ARENA])

        class Carver:
            def __init__(self, at=0):
                self.at = at

            def take(self, *shape):
                n = 1
                for s in shape:
                    n *= s
                assert self.at + n <= ARENA, "arena"
                v = arena[:, self.at:self.at + n]
                self.at += n
                if len(shape) == 2:
                    v = v.rearrange("p (a b) -> p a b", a=shape[0])
                if len(shape) == 3:
                    v = v.rearrange("p (a b c) -> p a b c", a=shape[0], b=shape[1])
                return v

        w_gcn = sb("w_gcn", [P, KT, HID])
        b_gcn_col = sb("b_gcn_col", [P, 1])
        w_fc_rows = sb("w_fc_rows", [P, KT, HID])[:, :, :]
        c = Carver()
        w_qkv = c.take(KT, 3 * D)
        w_fcT = c.take(D)
        bias_fc = c.take(D)
        shared_at = c.at
        xt = c.take(RING, D)
        ht = c.take(RING, D)
        hT = c.take(2, D)
        xg_out = c.take(RING, HID)
        c = Carver(shared_at)
        xg_in = c.take(LONG, 2, HID)
        onehot_w = c.take(LONG, 2, P)
        block_sum = c.take(GROUP, P)
        hidden = c.take(P)
        x_in = c.take(D)
        x1 = c.take(D)
        h1 = c.take(D)
        h1T = c.take(D)
        kv_out = c.take(2 * D)

        c = Carver()
        kv_in = c.take(RING, 2, 2 * D)
        onehot = c.take(RING, 2, P)
        onehotT = c.take(2, 2, P)
        message_at = c.take(RING, 2, AW)
        message = message_at.rearrange("p r t (h w) -> p r t h w", h=HEADS)
        product = c.take(2, 2, D)
        score = c.take(2, 2, HEADS)

        c = Carver()
        x1_in = c.take(ROWS, D)
        h1_in = c.take(ROWS, D)
        square = c.take(RING, D)
        recip_z = c.take(NB, HEADS)
        mean_b = c.take(D)
        scale_b = c.take(D)
        gamma_b = c.take(D)
        beta_b = c.take(D)

        class TableCarver(Carver):
            def take(self, *shape, dt=f32):
                n = 1
                for s in shape:
                    n *= s
                v = att[:, self.at:self.at + n]
                self.at += n
                if dt != f32:
                    v = v.bitcast(dt)
                if len(shape) == 2:
                    v = v.rearrange("p (a b) -> p a b", a=shape[0])
                return v

        c = TableCarver()
        dst_raw = c.take(NG, CHUNK, dt=i32)
        src_raw = c.take(NG, CHUNK, dt=i32)
        dst_rows = c.take(NG, CHUNK)
        src_rows = c.take(NG, CHUNK)
        w_rows = c.take(NG, CHUNK)
        slot_no = c.take(NS)
        chunk_of = c.take(NS)
        block_f = c.take(NS)
        block_base = c.take(NS)
        chunk_no = c.take(NG)
        chunk_end = c.take(NG)
        block_start = c.take(NB - 1)
        passed = c.take(NG, NB - 1)
        blocks_passed = c.take(NG)
        later = c.take(NG, NS)
        selects = c.take(NG, NS)
        partition_no = c.take(1)
        next_raw = c.take(NG, CHUNK, dt=i32)
        falls = c.take(NG, CHUNK)
        fall_count = c.take(1)
        rank = c.take(NG, CHUNK)
        rank_int = c.take(NG, CHUNK, dt=i32)
        threshold = c.take(NG, CHUNK)
        smaller = c.take(NG, CHUNK)
        own_offset = c.take(NG, CHUNK)
        edge_in_chunk = c.take(1, CHUNK)
        row_raw = c.take(CHUNK, dt=i32)
        row_key = c.take(CHUNK)
        at = c.at
        compared = c.take(COLUMNS, CHUNK)
        end_rows = TableCarver(at).take(3, NS)
        assert 3 * NS <= COLUMNS * CHUNK
        is_own = c.take(NG)
        is_later = c.take(NG)
        staged = [c.take(1, dt=i32) for _ in range(4)]
        assert c.at <= (NB + 1) * AW

        bank = ctx.enter_context(nc.psum_tensor("bank", [P, 8, 512], f32))

        edges_in = sem("edges_in")
        order_counted = sem("order_counted")
        order_summed = sem("order_summed")
        order_known = sem("order_known")
        dst_stored = sem("dst_stored")
        row_in = sem("row_in")
        row_read = sem("row_read")
        ranked = sem("ranked")
        column_staged = sem("column_staged")
        column_out = [sem(f"column_out{n}") for n in range(3)]
        reordered = sem("reordered")
        edges_final = sem("edges_final")
        weights_in = sem("weights_in")
        padded = sem("padded")
        iotas = sem("iotas")
        vec = sem("vec")
        consts_ready = sem("consts_ready")
        later_ready = sem("later_ready")
        chunk_counted = sem("chunk_counted")
        selects_ready = sem("selects_ready")
        tables_in_psum = sem("tables_in_psum")
        tables_ready = sem("tables_ready")
        fcT_in_psum = sem("fcT_in_psum")
        fcT_ready = sem("fcT_ready")
        w_qkv_in = sem("w_qkv_in")
        act_go = sem("act_go")
        pool_go = sem("pool_go")
        pe_go = sem("pe_go")
        sp_go = sem("sp_go")
        vec_go = sem("vec_go")

        class NodeSems:
            def __init__(self, tag):
                self.x_in = [sem(f"{tag}_x_in{r}") for r in range(RING)]
                self.stats_done = sem(f"{tag}_stats_done")
                self.aggr_done = sem(f"{tag}_aggr_done")
                self.var_ready = sem(f"{tag}_var_ready")
                self.std_ready = sem(f"{tag}_std_ready")
                self.scale_ready = sem(f"{tag}_scale_ready")
                self.norm_ready = sem(f"{tag}_norm_ready")
                self.h_ready = sem(f"{tag}_h_ready")
                self.turned = sem(f"{tag}_turned")
                self.hT_ready = sem(f"{tag}_hT_ready")
                self.projected = sem(f"{tag}_projected")
                self.evacuated = sem(f"{tag}_evacuated")
                self.stored = [sem(f"{tag}_stored{r}") for r in range(RING)]

        n0 = NodeSems("n0")
        turned = sem("turned")
        projected = sem("projected")
        kv_projected = sem("kv_projected")
        h1_ready = sem("h1_ready")
        h1T_ready = sem("h1T_ready")
        x_back = sem("x_back")
        x_with_bias = sem("x_with_bias")
        x1_stats = sem("x1_stats")
        x1_aggr = sem("x1_aggr")
        x1_var_ready = sem("x1_var_ready")
        x1_std_ready = sem("x1_std_ready")
        x1_scale_ready = sem("x1_scale_ready")
        x1_norm_ready = sem("x1_norm_ready")
        v_evacuated = sem("v_evacuated")
        kv_stored = sem("kv_stored")
        kv_free = sem("kv_free")
        hidden_ready = sem("hidden_ready")
        fc_done = sem("fc_done")
        x1_ready = sem("x1_ready")
        q_evacuated = sem("q_evacuated")
        k_evacuated = sem("k_evacuated")
        rows_stored = sem("rows_stored")

        index_ready = sem("index_ready")
        xg_gathered = [sem(f"xg_gathered{r}") for r in range(LONG)]
        onehot_w_ready = sem("onehot_w_ready")
        summed = sem("summed")
        added = sem("added")

        index2_ready = sem("index2_ready")
        kv_gathered = [sem(f"kv_gathered{r}") for r in range(RING)]
        onehot_ready = sem("onehot_ready")
        onehot_turned = sem("onehot_turned")
        onehotT_ready = sem("onehotT_ready")
        queries_ready = sem("queries_ready")
        product_ready = sem("product_ready")
        score_ready = sem("score_ready")
        clipped = sem("clipped")
        weight_ready = sem("weight_ready")
        message0_ready = sem("message0_ready")
        message1_ready = sem("message1_ready")
        att_summed = sem("att_summed")
        att_added = sem("att_added")

        norm_in = sem("norm_in")
        h1_back = [sem(f"h1_back{r}") for r in range(ROWS)]
        x1_back = [sem(f"x1_back{r}") for r in range(ROWS)]
        attended = sem("attended")
        with_h = [sem(f"with_h{n}") for n in ("_even", "_odd")]
        mean_summed = sem("mean_summed")
        centered = sem("centered")
        squared = sem("squared")
        square_read = sem("square_read")
        var_summed = sem("var_summed")
        bn_var_ready = sem("bn_var_ready")
        bn_std_ready = sem("bn_std_ready")
        x1_biased = sem("x1_biased")
        scaled = sem("scaled")
        y_ready = sem("y_ready")
        y_stored = [sem(f"y_stored{r}") for r in range(ROWS)]

        block = ctx.enter_context(nc.Block())

        def load_chunks(engine, to, frm, length):
            full = length // CHUNK
            groups = full // P
            rest = full - groups * P
            odd = length - full * CHUNK
            if groups:
                engine.dma_start(to[:, 0:groups, :], frm[0:groups * P * CHUNK].rearrange(
                    "(g p k) -> p g k", g=groups, p=P)).then_inc(edges_in, 16)
            if rest:
                engine.dma_start(to[0:rest, groups, :], frm[groups * P * CHUNK:full * CHUNK].rearrange(
                    "(p k) -> p k", k=CHUNK)).then_inc(edges_in, 16)
            if odd:
                engine.dma_start(to[rest:rest + 1, groups, 0:odd],
                                 frm[full * CHUNK:length].rearrange("(p k) -> p k", p=1)).then_inc(edges_in, 16)
            return (groups > 0) + (rest > 0) + (odd > 0)

        loads = []

        def node_rows(t, n):
            if isinstance(n, int):
                return t[n * P:min(N, (n + 1) * P), :] if t is x or t is out else t[n * P:(n + 1) * P, :]
            return t[bass.ds(n * P, P), :]

        def used(t, n, tile):
            if isinstance(n, int) and (t is x or t is out):
                return tile[0:min(P, N - n * P)]
            return tile

        def message_of(it, t):
            to = message[:, it.r, t, :, :]
            return (to[:, :, 0:DH], kv_in[:, it.r, t, D:2 * D].rearrange("p (h d) -> p h d", h=HEADS),
                    to[:, :, DH:DH + 1].broadcast_to([P, HEADS, DH]))

        def slot_column(table, it, t=None):
            flat = table[:, :, :].rearrange("p j t -> p (j t)")
            at, n = (it.n * 2, 2) if t is None else (it.n * 2 + t, 1)
            return flat[:, at:at + n] if it.fixed else flat[:, bass.ds(at, n)]

        def slot_scalar(table, it):
            return table[:, it.n:it.n + 1] if it.fixed else table[:, bass.ds(it.n, 1)]

        def wait_with_h(engine, it, back=0):
            if not it.fixed or it.n >= back:
                engine.wait_ge(with_h[it.r % 2], it.turn * (ROWS // 2) + (it.r // 2 + 1 - back // 2))

        def slot_finish(engine, it):
            at = finished[0:1, it.n:it.n + 1] if it.fixed else finished[0:1, bass.ds(it.n, 1)]
            return engine.value_load(at, min_val=0, max_val=MODULUS ** GROUP - 1)

        def each_finished(engine, it, block_end):
            if not it.exists or not (it.r % GROUP == GROUP - 1 or (it.fixed and it.n == NS - 1)):
                return
            digits = slot_finish(engine, it)
            with engine.If(digits > 0):
                for i in range(it.r % GROUP + 1):
                    blocks = engine.snap(digits // MODULUS ** i % MODULUS)
                    with engine.If(blocks > 0):
                        block_end(blocks, i)

        def each_counted(engine, it, block_end):
            if not it.exists or not (it.r % GROUP == GROUP - 1 or (it.fixed and it.n == NS - 1)):
                return
            at = group_ends[0:1, it.n:it.n + 1] if it.fixed else group_ends[0:1, bass.ds(it.n, 1)]
            ends = engine.value_load(at, min_val=0, max_val=COUNTS * (NB + 1) - 1)

            def rest(k):
                if k <= it.r % GROUP:
                    with engine.If(ends % COUNTS > k):
                        block_end(engine.snap(ends // COUNTS + k))
                        rest(k + 1)

            with engine.If(ends > 0):
                block_end(engine.snap(ends // COUNTS))
                rest(1)

        def before_last(blocks, back=1):
            return nc.s_assert_within((blocks + (MODULUS - back)) % MODULUS, 1, NB - 1)

        def slot_block(engine, it):
            at = block_of[0:1, it.n:it.n + 1] if it.fixed else block_of[0:1, bass.ds(it.n, 1)]
            return engine.value_load(at, min_val=0, max_val=NB - 1)

        @block.sync
        def _(sp):
            sp.wait_ge(padded, 4)
            loads.append(load_chunks(sp, dst_raw, dst, E) + load_chunks(sp, next_raw, dst[1:E], E - 1)
                         + load_chunks(sp, src_raw, src, E) + load_chunks(sp, w_rows, edge_weight, E))
            sp.dma_start(w_gcn[:, :, :], W_gcn.rearrange("(k p) n -> p k n", p=P)).then_inc(weights_in, 16)
            sp.dma_start(w_fc_rows, W_fc.rearrange("(k p) n -> p k n", p=P)).then_inc(weights_in, 16)
            sp.dma_start(b_gcn_col[:, :], b_gcn.rearrange("(p a) -> p a", a=1)).then_inc(weights_in, 16)
            sp.dma_start(bias_fc, b_fc.rearrange("(a n) -> a n", a=1).broadcast_to([P, D])).then_inc(weights_in, 16)
            for i, w in enumerate((Wq, Wk, Wv)):
                sp.dma_start(w_qkv[:, :, i * D:(i + 1) * D],
                             w.rearrange("(k p) n -> p k n", p=P)).then_inc(w_qkv_in, 16)

            def step0(turn, place):
                it = Item(turn, place, 3, NB)
                if it.exists:
                    it.wait(sp, n0.h_ready, back=RING)
                    sp.sem_inc(sp_go, 1)
                    sp.dma_start(used(x, it.n, xt[:, it.r, :]), node_rows(x, it.n)).then_inc(n0.x_in[it.r], 16)
                it = Item(turn, place, -5, NB)
                if it.exists:
                    it.wait(sp, n0.evacuated)
                    sp.sem_inc(sp_go, 1)
                    sp.dma_start(node_rows(xg_dram, it.n), xg_out[:, it.r, :]).then_inc(n0.stored[it.r], 16)

            run_steps(sp, NB, 3, 5, step0)

            for r in range(RING):
                sp.wait_ge(n0.stored[r], 16 * len(range(r, NB, RING)))
            sp.sem_inc(kv_free, 1)

            def step1(turn, place):
                it = Item(turn, place, 1, NB)
                if it.exists:
                    it.wait(sp, x1_ready, back=1)
                    sp.sem_inc(sp_go, 1)
                    sp.dma_start(used(x, it.n, x_in), node_rows(x, it.n)).then_inc(x_back, 16)
                it = Item(turn, place, 0, NB)
                if it.exists:
                    it.wait(sp, h1_ready)
                    sp.sem_inc(sp_go, 1)
                    sp.dma_start(node_rows(x1_dram, it.n), x1).then_inc(rows_stored, 16)
                    sp.dma_start(node_rows(h1_dram, it.n), h1).then_inc(rows_stored, 16)
                it = Item(turn, place, -1, NB)
                if it.exists:
                    it.wait(sp, v_evacuated)
                    sp.sem_inc(sp_go, 1)
                    it.wait(sp, k_evacuated)
                    sp.sem_inc(sp_go, 1)
                    sp.dma_start(node_rows(kv_dram, it.n), kv_out).then_inc(kv_stored, 16)
                    it.wait(sp, kv_stored, per=16)
                    sp.sem_inc(kv_free, 1)

            run_steps(sp, NB, 1, 1, step1)

            sp.wait_ge(att_added, NS)
            sp.wait_ge(rows_stored, 32 * NB)
            sp.dma_start(gamma_b, gamma.rearrange("(a n) -> a n", a=1).broadcast_to([P, D])).then_inc(norm_in, 16)
            sp.dma_start(beta_b, beta.rearrange("(a n) -> a n", a=1).broadcast_to([P, D])).then_inc(norm_in, 16)

            def step_h(turn, place):
                it = Item(turn, place, 6, NB, ROWS)
                if it.exists:
                    wait_with_h(sp, it, back=ROWS)
                    sp.sem_inc(sp_go, 1)
                    sp.dma_start(h1_in[:, it.r, :], node_rows(h1_dram, it.n)).then_inc(h1_back[it.r], 16)

            run_steps(sp, NB, 6, 0, step_h, ROWS)

            def step_y(turn, place):
                it = Item(turn, place, 5, NB, ROWS)
                if it.exists:
                    it.wait_ring(sp, y_stored, 16, back=1)
                    sp.sem_inc(sp_go, 1)
                    sp.dma_start(x1_in[:, it.r, :], node_rows(x1_dram, it.n)).then_inc(x1_back[it.r], 16)
                it = Item(turn, place, 0, NB, ROWS)
                if it.exists:
                    it.wait(sp, y_ready)
                    sp.sem_inc(sp_go, 1)
                    sp.dma_start(node_rows(out, it.n), used(out, it.n, x1_in[:, it.r, :])).then_inc(y_stored[it.r], 16)

            run_steps(sp, NB, 5, 0, step_y, ROWS)
            for r in range(ROWS):
                sp.wait_ge(y_stored[r], 16 * len(range(r, NB, ROWS)))

        @block.gpsimd
        def _(pool):
            nc.gpsimd.memset(dst_raw, NONE).then_inc(padded, 1)
            nc.gpsimd.memset(next_raw, NONE).then_inc(padded, 1)
            nc.gpsimd.memset(src_raw, 0).then_inc(padded, 1)
            nc.gpsimd.memset(w_rows, 0.0).then_inc(padded, 1)
            free = dict(allow_small_or_imprecise_dtypes=True)
            nc.gpsimd.iota(column[:, :], pattern=[[1, P]], base=0, channel_multiplier=0, **free).then_inc(iotas, 1)
            nc.gpsimd.iota(partition_no, pattern=[[0, 1]], base=0, channel_multiplier=1, **free).then_inc(iotas, 1)
            nc.gpsimd.iota(slot_no, pattern=[[1, NS]], base=0, channel_multiplier=0, **free).then_inc(iotas, 1)
            nc.gpsimd.iota(chunk_no, pattern=[[P, NG]], base=0, channel_multiplier=1, **free).then_inc(iotas, 1)
            nc.gpsimd.iota(block_start, pattern=[[P, NB - 1]], base=P, channel_multiplier=0, **free).then_inc(iotas, 1)

            nc.gpsimd.iota(edge_in_chunk, pattern=[[0, 1], [1, CHUNK]], base=0, channel_multiplier=0,
                           **free).then_inc(iotas, 1)

            pool.wait_ge(order_known, 1)
            pool.wait_ge(edges_in, 16 * loads[0])
            unsorted = pool.value_load(out_of_order[0:1, 0:1], min_val=0, max_val=1)
            with pool.If(unsorted > 0):
                pool.dma_start(dst_padded.rearrange("(g p) k -> p g k", p=P), dst_raw).then_inc(dst_stored, 16)
                pool.wait_ge(dst_stored, 16)
                with pool.Fori(0, NG * P) as row:
                    pool.wait_ge(row_read, row + 1)
                    pool.sem_inc(pool_go, 1)
                    pool.dma_start(row_raw, dst_padded[bass.ds(row, 1), :].broadcast_to([P, CHUNK])).then_inc(row_in, 16)
                pool.wait_ge(ranked, 1)
                with pool.Fori(0, NG * CHUNK) as col:
                    for to, frm in zip(staged, (rank_int, dst_raw, src_raw, w_rows.bitcast(i32))):
                        last = nc.gpsimd.tensor_copy(to, frm.rearrange("p g k -> p (g k)")[:, bass.ds(col, 1)])
                    last.then_inc(column_staged, 1)
                    pool.wait_ge(column_staged, col + 1)
                    pool.sem_inc(pool_go, 1)
                    for to, frm, out_sem in zip(ordered, staged[1:], column_out):
                        pool.indirect_dma_start(out=to, out_offset=bass.IndirectOffsetOnAxis(ap=staged[0], axis=0),
                                                in_=frm, in_offset=None).then_inc(out_sem, 16)
                    for out_sem in column_out:
                        pool.wait_ge(out_sem, col * 16 + 16)
                        pool.sem_inc(pool_go, 1)
                for to, frm in zip((dst_raw, src_raw, w_rows.bitcast(i32)), ordered):
                    pool.dma_start(to, frm.rearrange("(g p k) a -> p g (k a)", g=NG, p=P)).then_inc(reordered, 16)
                pool.wait_ge(reordered, 48)
            pool.sem_inc(edges_final, 1)

            for r in range(RING):
                pool.wait_ge(n0.stored[r], 16 * len(range(r, NB, RING)))

            def gather0(turn, place):
                it = Item(turn, place, 0, NS, LONG)
                it.wait(pool, index_ready)
                it.wait(pool, summed, back=LONG)
                pool.sem_inc(pool_go, 1)
                for t in range(2):
                    pool.indirect_dma_start(
                        out=xg_in[:, it.r, t, :], out_offset=None, in_=xg_dram,
                        in_offset=bass.IndirectOffsetOnAxis(ap=gather_rows[:, it.r, t:t + 1], axis=0),
                    ).then_inc(xg_gathered[it.r], 16)

            run_steps(pool, NS, 0, 0, gather0, LONG)

            pool.wait_ge(kv_stored, 16 * NB)
            pool.wait_ge(rows_stored, 32 * NB)

            def gather_kv(it, t):
                pool.indirect_dma_start(
                    out=kv_in[:, it.r, t, :], out_offset=None, in_=kv_dram,
                    in_offset=bass.IndirectOffsetOnAxis(ap=gather_rows[:, it.r, t:t + 1], axis=0),
                ).then_inc(kv_gathered[it.r], 16)

            def step2(turn, place):
                ahead = Item(turn, place, 3, NS)
                it = Item(turn, place, 0, NS)
                if it.exists:
                    it.wait(pool, score_ready)
                    pool.sem_inc(pool_go, 1)
                    flat = score[:, it.r % 2, :, :]
                    limit = CLIP * DH ** 0.5
                    nc.gpsimd.tensor_scalar(flat, flat, limit, -limit, ALU.min, ALU.max).then_inc(clipped, 1)
                if ahead.exists:
                    ahead.wait(pool, index2_ready)
                    ahead.wait(pool, message1_ready, back=RING)
                    ahead.wait(pool, message0_ready, back=RING)
                    pool.sem_inc(pool_go, 1)
                    gather_kv(ahead, 0)
                    gather_kv(ahead, 1)
                if it.exists:
                    it.wait(pool, weight_ready)
                    it.wait(pool, att_summed, back=RING)
                    nc.gpsimd.tensor_tensor(*message_of(it, 0), ALU.mult).then_inc(message0_ready, 1)

            run_steps(pool, NS, 3, 0, step2)

            def attend_odd(turn, place):
                it = Item(turn, place, 0, NB, ROWS)
                if it.r % 2 == 1:
                    it.wait_ring(pool, h1_back, 16)
                    pool.sem_inc(pool_go, 1)
                    it.wait(pool, attended)
                    pool.sem_inc(pool_go, 1)
                    to = att[:, it.n * AW:it.n * AW + D] if it.fixed else att[:, bass.ds(it.n * AW, D)]
                    nc.gpsimd.tensor_tensor(to, square[:, it.r % RING, :], h1_in[:, it.r, :],
                                            ALU.add).then_inc(with_h[1], 1)

            run_steps(pool, NB, 0, 0, attend_odd, ROWS)

            pool.wait_ge(norm_in, 32)

            def bias2(turn, place):
                it = Item(turn, place, 2, NB, ROWS)
                if it.exists:
                    it.wait_ring(pool, x1_back, 16)
                    nc.gpsimd.tensor_tensor(x1_in[:, it.r, :], x1_in[:, it.r, :], beta_b, ALU.add).then_inc(x1_biased, 1)

            run_steps(pool, NB, 2, 0, bias2, ROWS)

        def node_act(act, s, turn, place):
            it = Item(turn, place, 0, NB)
            if it.exists:
                it.wait(act, s.var_ready)
                nc.scalar.activation(scale[:, it.r:it.r + 1], spread[:, it.r:it.r + 1], ACT.Sqrt).then_inc(s.std_ready, 1)
            it = Item(turn, place, -1, NB)
            if it.exists:
                it.wait(act, s.norm_ready)
                it.wait(act, s.turned, back=RING)
                nc.scalar.activation(ht[:, it.r, :], xt[:, it.r, :], ACT.Relu, bias=shift[:, it.r:it.r + 1],
                                     scale=scale[:, it.r:it.r + 1]).then_inc(s.h_ready, 1)
            it = Item(turn, place, -2, NB)
            if it.exists:
                it.wait(act, s.turned)
                it.wait(act, s.projected, back=2)
                nc.scalar.activation(hT[:, it.r % 2, :], bank[:, it.r % 2, :],
                                     ACT.Copy).then_inc(s.hT_ready, 1)

        @block.scalar
        def _(act):
            run_steps(act, NB, 0, 2, lambda turn, place: node_act(act, n0, turn, place))

            act.wait_ge(tables_ready, 1)

            act.wait_ge(weights_in, 64)

            def attention_rows(count):
                act.wait_ge(kv_projected, count)
                act.sem_inc(act_go, 1)
                act.wait_ge(kv_free, count)
                nc.scalar.activation(kv_out[:, 0:D], bank[:, 5, :], ACT.Copy).then_inc(k_evacuated, 1)
                act.wait_ge(projected, count)
                act.sem_inc(act_go, 1)
                fixed = isinstance(count, int)
                to = att[:, count * AW:count * AW + D] if fixed else att[:, bass.ds(count * AW, D)]
                nc.scalar.activation(to, bank[:, 4, :], ACT.Copy).then_inc(q_evacuated, 1)

            def turned_rows(count):
                act.wait_ge(turned, count)
                nc.scalar.activation(h1T, bank[:, 3, :], ACT.Copy).then_inc(h1T_ready, 1)

            def edges0(turn, place):
                it = Item(turn, place, LONG, NS, LONG)
                if it.exists:
                    it.wait_ring(act, xg_gathered, 32, back=1)
                    act.sem_inc(act_go, 1)
                    nc.scalar.activation(gather_rows[:, it.r, :], slot_column(rows_of, it),
                                         ACT.Copy).then_inc(index_ready, 1)
                it = Item(turn, place, -1, NS, LONG)

                def block_end(blocks, i):
                    it.wait(act, added)
                    nc.scalar.activation(hidden, block_sum[:, i, :], ACT.Identity,
                                         bias=b_gcn_col[:, :]).then_inc(hidden_ready, 1)
                    with act.If(blocks > 2):
                        attention_rows(before_last(blocks, 2))
                    with act.If(blocks > 1):
                        turned_rows(before_last(blocks))
                    act.wait_ge(x1_var_ready, blocks)
                    nc.scalar.activation(scale[:, 0:1], spread[:, 0:1], ACT.Sqrt).then_inc(x1_std_ready, 1)
                    act.wait_ge(x1_norm_ready, blocks)
                    nc.scalar.activation(h1, x1, ACT.Relu, bias=shift[:, 0:1],
                                         scale=scale[:, 0:1]).then_inc(h1_ready, 1)

                each_finished(act, it, block_end)

            run_steps(act, NS, LONG, 1, edges0, LONG)
            attention_rows(NB - 1)
            turned_rows(NB)
            attention_rows(NB)

            act.wait_ge(kv_stored, 16 * NB)
            act.wait_ge(rows_stored, 32 * NB)

            def second_tile(it, heads):
                for h in heads:
                    last = nc.scalar.activation(message[:, it.r, 1, h, 0:DH],
                                                kv_in[:, it.r, 1, D + h * DH:D + (h + 1) * DH], ACT.Copy,
                                                scale=message[:, it.r, 1, h, DH:DH + 1])
                return last

            def step2(turn, place):
                it = Item(turn, place, 1, NS)
                if it.exists:
                    it.wait(act, onehot_turned)
                    it.wait(act, queries_ready, back=2)
                    nc.scalar.activation(onehotT[:, it.r % 2, :, :], bank[:, 6 + it.r % 2, 0:CHUNK].rearrange(
                        "p (t e) -> p t e", t=2), ACT.Copy).then_inc(onehotT_ready, 1)
                it = Item(turn, place, -1, NS)
                if it.exists:
                    second_tile(it, range(HEADS // 2, HEADS)).then_inc(message1_ready, 1)
                it = Item(turn, place, 4, NS)
                if it.exists:
                    it.wait_ring(act, kv_gathered, 32, back=1)
                    act.sem_inc(act_go, 1)
                    nc.scalar.activation(gather_rows[:, it.r, :], slot_column(rows_of, it),
                                         ACT.Copy).then_inc(index2_ready, 1)
                it = Item(turn, place, 0, NS)
                if it.exists:
                    it.wait(act, clipped)
                    it.wait(act, att_summed, back=RING)
                    nc.scalar.activation(message[:, it.r, :, :, DH], score[:, it.r % 2, :, :], ACT.Exp,
                                         scale=DH ** -0.5).then_inc(weight_ready, 1)
                    it.wait(act, weight_ready)
                    second_tile(it, range(0, HEADS // 2))

            run_steps(act, NS, 4, 1, step2)

            def squares(turn, place):
                it = Item(turn, place, 0, NB)
                it.wait(act, centered)
                it.wait(act, square_read, back=RING)
                act.sem_inc(act_go, 1)
                at = it.n * AW
                nc.scalar.activation(square[:, it.r, :], att[:, at:at + D] if it.fixed else att[:, bass.ds(at, D)],
                                     ACT.Square).then_inc(squared, 1)

            run_steps(act, NB, 0, 0, squares)
            act.wait_ge(bn_var_ready, 1)
            nc.scalar.activation(scale_b, scale_b, ACT.Sqrt).then_inc(bn_std_ready, 1)

        def rank_edges(dve):
            flat = lambda t: t.rearrange("p g k -> p (g k)")
            nc.vector.memset(rank, 0.0)
            nc.vector.tensor_copy(dst_rows, dst_raw)
            dve.drain()
            dve.sem_inc(row_read, 1)
            with dve.Fori(0, NG * P) as row:
                dve.wait_ge(row_in, row * 16 + 16)
                nc.vector.tensor_copy(row_key, row_raw)
                dve.drain()
                dve.sem_inc(row_read, 1)
                nc.vector.tensor_scalar(row_key, row_key, float(CHUNK), None, ALU.mult)
                dve.drain()
                nc.vector.tensor_tensor(row_key, row_key, edge_in_chunk[:, 0, :], ALU.add)
                nc.vector.tensor_scalar(is_own, chunk_no, row_number[:, 0:1], None, ALU.is_equal)
                nc.vector.tensor_scalar(is_later, chunk_no, row_number[:, 0:1], float(CHUNK), ALU.is_gt, ALU.mult)
                nc.vector.tensor_scalar(threshold, dst_rows, float(CHUNK), None, ALU.mult)
                dve.drain()
                for g in range(NG):
                    nc.vector.tensor_scalar(own_offset[:, g, :], edge_in_chunk[:, 0, :], is_own[:, g:g + 1],
                                            is_later[:, g:g + 1], ALU.mult, ALU.add)
                nc.vector.tensor_scalar(row_number[:, :], row_number[:, :], 1.0, None, ALU.add)
                dve.drain()
                nc.vector.tensor_tensor(threshold, threshold, own_offset, ALU.add)
                dve.drain()
                with dve.Fori(0, NG * CHUNK // COLUMNS) as group:
                    nc.vector.tensor_tensor(compared, row_key.unsqueeze(1).broadcast_to([P, COLUMNS, CHUNK]),
                                            flat(threshold)[:, bass.ds(group * COLUMNS, COLUMNS)].unsqueeze(2).broadcast_to(
                                                [P, COLUMNS, CHUNK]), ALU.is_lt)
                    dve.drain()
                    nc.vector.tensor_reduce(flat(smaller)[:, bass.ds(group * COLUMNS, COLUMNS)], compared, AX.X, ALU.add)
                    dve.drain()
                nc.vector.tensor_tensor(rank, rank, smaller, ALU.add)
                dve.drain()
            nc.vector.tensor_copy(rank_int, rank)
            dve.drain()
            dve.sem_inc(ranked, 1)

        @block.vector
        def _(dve):
            steps = [0]

            def link(instruction):
                steps[0] += 1
                instruction.then_inc(vec, 1)
                dve.wait_ge(vec, steps[0])

            nc.vector.memset(ones[:, :], 1.0)
            link(nc.vector.memset(row_number[:, :], 0.0))
            dve.wait_ge(iotas, 6)
            nc.vector.tensor_scalar(ident[:, :], column[:, :], partition_no, None, ALU.is_equal).then_inc(consts_ready, 1)

            dve.wait_ge(edges_in, 16 * loads[0])
            nc.vector.tensor_tensor(falls, next_raw, dst_raw, ALU.is_lt).then_inc(order_counted, 1)
            dve.wait_ge(order_counted, 1)
            nc.vector.tensor_reduce(fall_count, falls.rearrange("p g k -> p (g k)"), AX.X, ALU.add).then_inc(order_counted, 1)
            dve.wait_ge(order_summed, 1)
            link(nc.vector.tensor_scalar(out_of_order[:, :], bank[0:1, 0, 0:1], 1.0, None, ALU.min))
            dve.sem_inc(order_known, 1)
            unsorted = dve.value_load(out_of_order[0:1, 0:1], min_val=0, max_val=1)
            with dve.If(unsorted > 0):
                rank_edges(dve)
            dve.wait_ge(edges_final, 1)
            nc.vector.tensor_copy(src_rows, src_raw)
            link(nc.vector.tensor_copy(dst_rows, dst_raw))
            last_dst = dst_rows[:, :, CHUNK - 1:CHUNK]
            link(nc.vector.tensor_tensor(passed, last_dst.broadcast_to([P, NG, NB - 1]),
                                         block_start.unsqueeze(1).broadcast_to([P, NG, NB - 1]), ALU.is_ge))
            link(nc.vector.tensor_reduce(blocks_passed, passed, AX.X, ALU.add))
            link(nc.vector.tensor_tensor(chunk_end, blocks_passed, chunk_no, ALU.add))
            for g in range(NG):
                last = nc.vector.tensor_scalar(later[:, g, :], slot_no, chunk_end[:, g:g + 1], None, ALU.is_gt)
            last.then_inc(later_ready, 1)
            dve.wait_ge(chunk_counted, 1)
            link(nc.vector.tensor_copy(chunk_of, bank[:, 0, 0:NS]))
            for g in range(NG):
                last = nc.vector.tensor_scalar(selects[:, g, :], chunk_of, chunk_no[:, g:g + 1], None, ALU.is_equal)
            last.then_inc(selects_ready, 1)
            link(nc.vector.tensor_tensor(block_f, slot_no, chunk_of, ALU.subtract))
            nc.vector.tensor_scalar(block_base, block_f, float(P), None, ALU.mult)
            nc.vector.tensor_copy(block_of[:, :], block_f[0:1, :])
            nc.vector.memset(same_block[:, 0:1], 0.0)
            link(nc.vector.tensor_tensor(same_block[:, 1:NS], block_f[:, 1:NS], block_f[:, 0:NS - 1], ALU.is_equal))
            block_row, same_row, ends_row = block_f[0:1, :], same_block[0:1, :], later[0:1, 0, 0:NS]
            nc.vector.memset(ends_row[:, NS - 1:NS], 1.0)
            link(nc.vector.tensor_scalar(ends_row[:, 0:NS - 1], same_row[:, 1:NS], -1.0, 1.0, ALU.mult, ALU.add))
            count_row, total_row, any_row = (end_rows[0:1, n, :] for n in range(3))
            nc.vector.tensor_copy(count_row, ends_row)
            link(nc.vector.tensor_tensor(total_row, block_row, ends_row, ALU.add))
            for i in range(1, GROUP):
                n = len(range(i, NS, GROUP))
                link(nc.vector.tensor_tensor(count_row[:, i:NS:GROUP], count_row[:, i:NS:GROUP],
                                             count_row[:, i - 1:i - 1 + (n - 1) * GROUP + 1:GROUP], ALU.add))
            nc.vector.tensor_scalar(any_row, count_row, 1.0, None, ALU.min)
            link(nc.vector.tensor_scalar(total_row, total_row, 1.0, float(COUNTS), ALU.add, ALU.mult))
            link(nc.vector.scalar_tensor_tensor(total_row, count_row, 1.0 - COUNTS, total_row, ALU.mult, ALU.add))
            link(nc.vector.tensor_tensor(group_ends[:, :], total_row, any_row, ALU.mult))
            link(nc.vector.scalar_tensor_tensor(ends_row, block_row, 1.0, ends_row, ALU.add, ALU.mult))
            for i in range(1, GROUP):
                n = len(range(i, NS, GROUP))
                link(nc.vector.scalar_tensor_tensor(ends_row[:, i:NS:GROUP], ends_row[:, i:NS:GROUP], float(MODULUS ** i),
                                                    ends_row[:, i - 1:i - 1 + (n - 1) * GROUP + 1:GROUP],
                                                    ALU.mult, ALU.add))
            link(nc.vector.tensor_copy(finished[:, :], ends_row))
            dve.wait_ge(tables_in_psum, 1)
            for t in range(2):
                nc.vector.tensor_tensor(dst_in_block[:, :, t], bank[:, 1 + t, 0:NS], block_base, ALU.subtract)
                nc.vector.tensor_copy(rows_of[:, :, t], bank[:, 3 + t, 0:NS])
                last = nc.vector.tensor_copy(weight_of[:, :, t], bank[:, 5 + t, 0:NS])
            last.then_inc(tables_ready, 1)
            dve.wait_ge(tables_ready, 1)
            dve.wait_ge(fcT_in_psum, 1)
            nc.vector.tensor_copy(w_fcT, bank[:, 7, :]).then_inc(fcT_ready, 1)

            def node_stats(s, turn, place):
                it = Item(turn, place, 0, NB)
                if it.exists:
                    it.wait_ring(dve, s.x_in, 16)
                    it.wait(dve, s.h_ready, back=RING)
                    nc.vector.bn_stats(stats[:, it.r, :], xt[:, it.r, :]).then_inc(s.stats_done, 1)
                    it.wait(dve, s.stats_done)
                    dve.sem_inc(vec_go, 1)
                    nc.vector.bn_aggr(mean_var[:, it.r, :], stats[:, it.r, :]).then_inc(s.aggr_done, 1)
                    it.wait(dve, s.aggr_done)
                    nc.vector.tensor_scalar(spread[:, it.r:it.r + 1], mean_var[:, it.r, 1:2], LN_EPS, None,
                                            ALU.add).then_inc(s.var_ready, 1)
                it = Item(turn, place, -1, NB)
                if it.exists:
                    it.wait(dve, s.std_ready)
                    nc.vector.reciprocal(scale[:, it.r:it.r + 1], scale[:, it.r:it.r + 1]).then_inc(s.scale_ready, 1)
                    it.wait(dve, s.scale_ready)
                    nc.vector.scalar_tensor_tensor(shift[:, it.r:it.r + 1], mean_var[:, it.r, 0:1], -1.0,
                                                   scale[:, it.r:it.r + 1], ALU.mult, ALU.mult).then_inc(s.norm_ready, 1)

            def step0(turn, place):
                node_stats(n0, turn, place)
                it = Item(turn, place, -4, NB)
                if it.exists:
                    it.wait(dve, n0.projected)
                    it.wait_ring(dve, n0.stored, 16, back=1)
                    nc.vector.tensor_copy(xg_out[:, it.r, :], bank[:, 2 + it.r, 0:HID]).then_inc(n0.evacuated, 1)

            run_steps(dve, NB, 0, 4, step0)
            sums = att[:, :].rearrange("p (b w) -> p b w", w=AW)
            nc.vector.memset(sums[:, :, D:AW], 0.0)
            link(nc.vector.memset(sums[:, 0:1, 0:D], 0.0))

            for r in range(RING):
                dve.wait_ge(n0.stored[r], 16 * len(range(r, NB, RING)))

            link(nc.vector.memset(block_sum.rearrange("p g n -> p (g n)"), 0.0))
            dve.wait_ge(weights_in, 64)

            def first_residual(blocks):
                dve.wait_ge(x_back, blocks * 16)
                nc.vector.tensor_tensor(x_in, x_in, bias_fc, ALU.add).then_inc(x_with_bias, 1)
                with dve.If(blocks > 1):
                    dve.wait_ge(rows_stored, before_last(blocks) * 32)
                    dve.sem_inc(vec_go, 1)
                dve.wait_ge(x_with_bias, blocks)
                dve.sem_inc(vec_go, 1)
                dve.wait_ge(fc_done, blocks)
                nc.vector.tensor_tensor(x1, x_in, bank[:, 2, :], ALU.add).then_inc(x1_ready, 1)
                dve.wait_ge(x1_ready, blocks)
                nc.vector.bn_stats(stats[:, 0, :], x1).then_inc(x1_stats, 1)
                dve.wait_ge(x1_stats, blocks)
                dve.sem_inc(vec_go, 1)
                nc.vector.bn_aggr(mean_var[:, 0, :], stats[:, 0, :]).then_inc(x1_aggr, 1)
                dve.wait_ge(x1_aggr, blocks)
                nc.vector.tensor_scalar(spread[:, 0:1], mean_var[:, 0, 1:2], LN_EPS, None,
                                        ALU.add).then_inc(x1_var_ready, 1)
                dve.wait_ge(x1_std_ready, blocks)
                nc.vector.reciprocal(scale[:, 0:1], scale[:, 0:1]).then_inc(x1_scale_ready, 1)
                dve.wait_ge(x1_scale_ready, blocks)
                nc.vector.scalar_tensor_tensor(shift[:, 0:1], mean_var[:, 0, 0:1], -1.0, scale[:, 0:1],
                                               ALU.mult, ALU.mult).then_inc(x1_norm_ready, 1)

            def values_out(count):
                dve.wait_ge(kv_free, count)
                dve.sem_inc(vec_go, 1)
                dve.wait_ge(kv_projected, count)
                nc.vector.tensor_copy(kv_out[:, D:2 * D], bank[:, 6, :]).then_inc(v_evacuated, 1)

            def edges0(turn, place):
                it = Item(turn, place, -1, NS, LONG)
                if it.exists:
                    it.wait(dve, summed)
                    it.wait(dve, added, back=1)
                    nc.vector.scalar_tensor_tensor(block_sum[:, it.r % GROUP, :], block_sum[:, (it.r - 1) % GROUP, :],
                                                   slot_scalar(same_block, it),
                                                   bank[:, it.r % 2, 0:P], ALU.mult, ALU.add).then_inc(added, 1)
                it = Item(turn, place, 3, NS, LONG)
                if it.exists:
                    it.wait(dve, summed, back=LONG)
                    for t in range(2):
                        last = nc.vector.tensor_scalar(onehot_w[:, it.r, t, :], column[:, :],
                                                       slot_column(dst_in_block, it, t), slot_column(weight_of, it, t),
                                                       ALU.is_equal, ALU.mult)
                    last.then_inc(onehot_w_ready, 1)

                def block_end(blocks):
                    with dve.If(blocks > 2):
                        values_out(before_last(blocks, 2))
                    first_residual(blocks)

                each_counted(dve, Item(turn, place, -1, NS, LONG), block_end)

            run_steps(dve, NS, 3, 1, edges0, LONG)
            values_out(NB - 1)
            values_out(NB)

            dve.wait_ge(kv_stored, 16 * NB)
            dve.wait_ge(rows_stored, 32 * NB)

            def step2(turn, place):
                b = None
                it = Item(turn, place, 0, NS)
                if it.exists:
                    it.wait(dve, weight_ready, back=2)
                    it.wait(dve, score_ready, back=2)
                    it.wait_ring(dve, kv_gathered, 32)
                    it.wait(dve, queries_ready)
                    at = 2 * (it.r % 2)
                    nc.vector.tensor_tensor(product[:, it.r % 2, :, :], kv_in[:, it.r, :, 0:D],
                                            bank[:, at:at + 2, :], ALU.mult).then_inc(product_ready, 1)
                    it.wait(dve, product_ready)
                    nc.vector.tensor_reduce(score[:, it.r % 2, :, :].rearrange("p t h -> p (t h)"),
                                            product[:, it.r % 2, :, :].rearrange("p t (h d) -> p (t h) d", h=HEADS),
                                            AX.X, ALU.add).then_inc(score_ready, 1)
                    before = Item(turn, place, -2, NS)
                    b = slot_block(dve, before) if before.exists else None
                it = Item(turn, place, 2, NS)
                if it.exists:
                    it.wait(dve, att_summed, back=RING)
                    for t in range(2):
                        last = nc.vector.tensor_scalar(onehot[:, it.r, t, :], column[:, :],
                                                       slot_column(dst_in_block, it, t), None, ALU.is_equal)
                    last.then_inc(onehot_ready, 1)
                it = Item(turn, place, -2, NS)
                if it.exists:
                    if not Item(turn, place, 0, NS).exists:
                        b = slot_block(dve, it)
                    it.wait(dve, att_summed)
                    it.wait(dve, att_added, back=1)
                    to = att[:, bass.ds(b * AW, AW)].rearrange("p (a w) -> p a w", a=2)
                    nc.vector.scalar_tensor_tensor(to, to, slot_scalar(same_block, it), bank[:, 4:6, 0:HALF],
                                                   ALU.mult, ALU.add).then_inc(att_added, 1)

            run_steps(dve, NS, 2, 2, step2)

            dve.wait_ge(att_added, NS)
            z = att[:, 0:NB * AW].rearrange("p (b h w) -> p b h w", h=HEADS, w=DH + 1)[:, :, :, DH]
            link(nc.vector.tensor_scalar(recip_z, z, Z_EPS, None, ALU.add))
            link(nc.vector.reciprocal(recip_z, recip_z))
            flat_z = recip_z.rearrange("p b h -> p (b h)")

            def row(it):
                return att[:, it.n * AW:it.n * AW + D] if it.fixed else att[:, bass.ds(it.n * AW, D)]

            def attend(turn, place):
                it = Item(turn, place, 0, NB, ROWS)
                v = att[:, it.n * AW:(it.n + 1) * AW] if it.fixed else att[:, bass.ds(it.n * AW, AW)]
                v = v.rearrange("p (h w) -> p h w", h=HEADS)[:, :, 0:DH]
                part = square[:, it.r % RING, :]
                at = it.n * HEADS
                rz = flat_z[:, at:at + HEADS] if it.fixed else flat_z[:, bass.ds(at, HEADS)]
                wait_with_h(dve, it, back=RING)
                nc.vector.tensor_tensor(part.rearrange("p (h d) -> p h d", h=HEADS), v,
                                        rz.unsqueeze(2).broadcast_to([P, HEADS, DH]), ALU.mult).then_inc(attended, 1)
                if it.r % 2 == 0:
                    it.wait_ring(dve, h1_back, 16)
                    it.wait(dve, attended)
                    nc.vector.tensor_tensor(row(it), part, h1_in[:, it.r, :], ALU.add).then_inc(with_h[0], 1)

            run_steps(dve, NB, 0, 0, attend, ROWS)
            dve.wait_ge(mean_summed, 1)
            link(nc.vector.tensor_scalar(mean_b, bank[:, 0, :], 1.0 / N, None, ALU.mult))

            def center(turn, place):
                it = Item(turn, place, 0, NB)
                nc.vector.tensor_tensor(row(it), row(it), mean_b, ALU.subtract).then_inc(centered, 1)

            run_steps(dve, NB, 0, 0, center)
            dve.wait_ge(var_summed, 1)
            nc.vector.tensor_scalar(scale_b, bank[:, 1, :], 1.0 / N, BN_EPS, ALU.mult, ALU.add).then_inc(bn_var_ready, 1)
            dve.wait_ge(bn_std_ready, 1)
            link(nc.vector.reciprocal(scale_b, scale_b))
            dve.wait_ge(norm_in, 32)
            link(nc.vector.tensor_tensor(scale_b, scale_b, gamma_b, ALU.mult))

            def finish(turn, place):
                it = Item(turn, place, 0, NB, ROWS)
                nc.vector.tensor_tensor(row(it), row(it), scale_b, ALU.mult).then_inc(scaled, 1)
                it.wait(dve, scaled)
                it.wait(dve, x1_biased)
                nc.vector.tensor_tensor(x1_in[:, it.r, :], row(it), x1_in[:, it.r, :], ALU.add).then_inc(y_ready, 1)

            run_steps(dve, NB, 0, 0, finish, ROWS)

        @block.tensor
        def _(pe):
            def turn_rows(s, it, to):
                for k in range(KT):
                    last = nc.tensor.transpose(to[:, k * P:(k + 1) * P], ht[:, it.r, k * P:(k + 1) * P], ident[:, :])
                last.then_inc(s.turned, 1)

            pe.wait_ge(order_counted, 2)
            nc.tensor.matmul(bank[:, 0, 0:1], ones[:, :], fall_count, start=True, stop=True).then_inc(order_summed, 1)

            pe.wait_ge(later_ready, 1)
            for g in range(NG):
                last = nc.tensor.matmul(bank[:, 0, 0:NS], ones[:, :], later[:, g, :], start=(g == 0), stop=(g == NG - 1))
            last.then_inc(chunk_counted, 1)
            pe.wait_ge(selects_ready, 1)
            for a, rows in enumerate((dst_rows, src_rows, w_rows)):
                for t in range(2):
                    for g in range(NG):
                        last = nc.tensor.matmul(bank[:, 1 + 2 * a + t, 0:NS], rows[:, g, t * P:(t + 1) * P],
                                                selects[:, g, :], start=(g == 0), stop=(g == NG - 1))
            last.then_inc(tables_in_psum, 1)
            pe.wait_ge(weights_in, 64)
            for k in range(KT):
                last = nc.tensor.transpose(bank[:, 7, k * P:(k + 1) * P], w_fc_rows[:, k, :], ident[:, :])
            last.then_inc(fcT_in_psum, 1)
            pe.wait_ge(tables_ready, 1)

            def step0(turn, place):
                it = Item(turn, place, -1, NB)
                if it.exists:
                    it.wait(pe, n0.h_ready)
                    it.wait(pe, n0.hT_ready, back=2)
                    turn_rows(n0, it, bank[:, it.r % 2, :])
                it = Item(turn, place, -2, NB)
                if it.exists:
                    it.wait(pe, n0.hT_ready)
                    it.wait(pe, n0.evacuated, back=RING)
                    for k in range(KT):
                        last = nc.tensor.matmul(bank[:, 2 + it.r, 0:HID], hT[:, it.r % 2, k * P:(k + 1) * P],
                                                w_gcn[:, k, :], start=(k == 0), stop=(k == KT - 1))
                    last.then_inc(n0.projected, 1)

            run_steps(pe, NB, 0, 2, step0)

            pe.wait_ge(n0.hT_ready, NB)
            pe.wait_ge(n0.evacuated, NB)
            pe.wait_ge(fcT_ready, 1)
            pe.wait_ge(w_qkv_in, 48)

            def banks_free(count):
                pe.wait_ge(q_evacuated, count)
                pe.sem_inc(pe_go, 1)
                pe.wait_ge(k_evacuated, count)
                pe.sem_inc(pe_go, 1)
                pe.wait_ge(v_evacuated, count)
                pe.sem_inc(pe_go, 1)

            def turn_h1(count):
                pe.wait_ge(h1_ready, count)
                for k in range(KT):
                    last = nc.tensor.transpose(bank[:, 3, k * P:(k + 1) * P], h1[:, k * P:(k + 1) * P], ident[:, :])
                last.then_inc(turned, 1)

            def project(count):
                pe.wait_ge(h1T_ready, count)
                for i, done in ((1, None), (2, kv_projected), (0, projected)):
                    for k in range(KT):
                        last = nc.tensor.matmul(bank[:, 4 + i, :], h1T[:, k * P:(k + 1) * P],
                                                w_qkv[:, k, i * D:(i + 1) * D], start=(k == 0), stop=(k == KT - 1))
                    if done is not None:
                        last.then_inc(done, 1)

            def edges0(turn, place):
                it = Item(turn, place, 0, NS, LONG)
                if it.exists:
                    it.wait_ring(pe, xg_gathered, 32)
                    it.wait(pe, onehot_w_ready)
                    it.wait(pe, added, back=2)
                    for t in range(2):
                        last = nc.tensor.matmul(bank[:, it.r % 2, 0:P], xg_in[:, it.r, t, :], onehot_w[:, it.r, t, :],
                                                start=(t == 0), stop=(t == 1))
                    last.then_inc(summed, 1)

                def block_end(blocks):
                    with pe.If(blocks > 1):
                        turn_h1(before_last(blocks))
                    pe.wait_ge(hidden_ready, blocks)
                    nc.tensor.matmul(bank[:, 2, :], hidden, w_fcT, start=True, stop=True).then_inc(fc_done, 1)
                    with pe.If(blocks > 1):
                        with pe.If(blocks > 2):
                            banks_free(before_last(blocks, 2))
                        project(before_last(blocks))

                each_counted(pe, Item(turn, place, -1, NS, LONG), block_end)

            run_steps(pe, NS, 0, 1, edges0, LONG)
            turn_h1(NB)
            banks_free(NB - 1)
            project(NB)
            pe.wait_ge(q_evacuated, NB)
            pe.wait_ge(k_evacuated, NB)
            pe.wait_ge(v_evacuated, NB)

            def step2(turn, place):
                it = Item(turn, place, 1, NS)
                if it.exists:
                    it.wait(pe, onehot_ready)
                    it.wait(pe, onehotT_ready, back=2)
                    for t in range(2):
                        last = nc.tensor.transpose(bank[:, 6 + it.r % 2, t * P:(t + 1) * P], onehot[:, it.r, t, :],
                                                   ident[:, :])
                    last.then_inc(onehot_turned, 1)
                it = Item(turn, place, -2, NS)
                if it.exists:
                    it.wait(pe, message0_ready)
                    it.wait(pe, message1_ready)
                    it.wait(pe, att_added, back=1)
                    for half in range(2):
                        for t in range(2):
                            last = nc.tensor.matmul(bank[:, 4 + half, 0:HALF], onehot[:, it.r, t, :],
                                                    message_at[:, it.r, t, half * HALF:(half + 1) * HALF],
                                                    start=(t == 0), stop=(t == 1))
                    last.then_inc(att_summed, 1)
                it = Item(turn, place, 1, NS)
                if it.exists:
                    b = slot_block(pe, it)
                    it.wait(pe, onehotT_ready)
                    it.wait(pe, product_ready, back=2)
                    for t in range(2):
                        last = nc.tensor.matmul(bank[:, 2 * (it.r % 2) + t, :], onehotT[:, it.r % 2, t, :],
                                                att[:, bass.ds((b + 1) * AW, D)], start=True, stop=True)
                    last.then_inc(queries_ready, 1)

            run_steps(pe, NS, 1, 2, step2)

            def row(it, k):
                return att[0:k, it.n * AW:it.n * AW + D] if it.fixed else att[0:k, bass.ds(it.n * AW, D)]

            def sum_rows(turn, place):
                it = Item(turn, place, 0, NB, ROWS)
                k = TAIL if it.fixed and it.n == NB - 1 else P
                wait_with_h(pe, it)
                last = nc.tensor.matmul(bank[:, 0, :], ones[0:k, :], row(it, k), start=(it.fixed and it.n == 0),
                                        stop=(it.fixed and it.n == NB - 1))
                if it.fixed and it.n == NB - 1:
                    last.then_inc(mean_summed, 1)

            run_steps(pe, NB, 0, 0, sum_rows, ROWS)

            def sum_squares(turn, place):
                it = Item(turn, place, 0, NB)
                k = TAIL if it.fixed and it.n == NB - 1 else P
                it.wait(pe, squared)
                last = nc.tensor.matmul(bank[:, 1, :], ones[0:k, :], square[0:k, it.r, :], start=(it.fixed and it.n == 0),
                                        stop=(it.fixed and it.n == NB - 1))
                last.then_inc(var_summed if it.fixed and it.n == NB - 1 else square_read, 1)

            run_steps(pe, NB, 0, 0, sum_squares)


_INS = ['x', 'src', 'dst', 'edge_weight', 'L0_gnn_W_gcn', 'L0_gnn_b_gcn', 'L0_gnn_W_fc', 'L0_gnn_b_fc',
        'L1_gnn_Wq', 'L1_gnn_Wk', 'L1_gnn_Wv', 'L1_gnn_bn_gamma', 'L1_gnn_bn_beta']


def kernel(**inputs):
    import numpy as _np
    import concourse.bacc as _bacc
    from concourse import mybir as _mybir
    from concourse.bass_utils import run_bass_kernel_spmd as _run

    nc = _bacc.Bacc("TRN2", target_bir_lowering=False, num_devices=1)
    arrays, args = {}, []
    for name in _INS:
        a = _np.ascontiguousarray(inputs[name])
        arrays[f"in_{name}_dram"] = a
        args.append(nc.dram_tensor(f"in_{name}_dram", a.shape, _mybir.dt.from_np(a.dtype), kind="ExternalInput").ap())
    shape = _np.shape(inputs['x'])
    args.append(nc.dram_tensor("out_0_dram", shape, _mybir.dt.float32, kind="ExternalOutput").ap())
    build_program(nc, *args)
    r = _run(nc, [arrays], core_ids=[0])
    return r.results[0]["out_0_dram"]
```
